# Optimizing a Trainium2 kernel written in Bass

```python
import numpy as np
import jax
import jax.numpy as jnp

def _softmax(x, axis=-1):
    return jax.nn.softmax(x, axis=axis)

def _gelu(x):
    return jax.nn.gelu(x, approximate=True)

def _silu(x):
    return jax.nn.silu(x)

def _sigmoid(x):
    return jax.nn.sigmoid(x)

def _layernorm(x, axis=-1, eps=1e-05):
    m = jnp.mean(x, axis=axis, keepdims=True)
    v = jnp.var(x, axis=axis, keepdims=True)
    return (x - m) / jnp.sqrt(v + eps)

def _scatter_add(tgt, idx, src, axis=0):
    return tgt.at[idx].add(src)

def _segment_sum(src, seg, n):
    return jax.ops.segment_sum(src, seg, n)
kernel_name = 'mk_sandwich_d1_jaxref_r8_6673c6'

def setup_inputs(seed: int=0):
    np.random.seed(seed)
    _w = jnp.asarray

    def _L0_attn_setup():
        import jax, jax.numpy as jnp
        import numpy as np
        N_FILTERS = 128
        N_HEADS = 16
        key = jax.random.key(seed)
        k1, k2, k3 = jax.random.split(key, 3)
        x = jax.random.normal(k1, (8, 128, N_FILTERS), dtype=jnp.float32)
        w_qkv = jax.random.normal(k2, (N_FILTERS, N_FILTERS * 3), dtype=jnp.float32) * (0.02 / N_FILTERS) ** 0.5
        w_out = jax.random.normal(k3, (N_FILTERS, N_FILTERS), dtype=jnp.float32) * (0.02 / N_FILTERS) ** 0.5
        return {'x': x, 'w_qkv': w_qkv, 'w_out': w_out}
    _L0_attn_in = _L0_attn_setup()

    def _L0_ffn_setup():
        import jax, jax.numpy as jnp
        import numpy as np
        B, S, D = (2, 128, 128)
        E, K, F, FS = (8, 2, 64, 128)
        key = jax.random.key(seed)
        ks = jax.random.split(key, 9)
        s = lambda k, shape, fan: jax.random.normal(k, shape, jnp.float32) * fan ** (-0.5)
        return {'x': jax.random.normal(ks[0], (B, S, D), jnp.float32), 'Wr': s(ks[1], (D, E), D), 'Wg': s(ks[2], (E, D, F), D), 'Wu': s(ks[3], (E, D, F), D), 'Wd': s(ks[4], (E, F, D), F), 'Sg': s(ks[5], (D, FS), D), 'Su': s(ks[6], (D, FS), D), 'Sd': s(ks[7], (FS, D), FS), 'expert_bias': jnp.zeros((E,), jnp.float32)}
    _L0_ffn_in = _L0_ffn_setup()
    _d = {'L0_attn_x': _L0_attn_in['x'], 'L0_attn_w_qkv': _L0_attn_in['w_qkv'], 'L0_attn_w_out': _L0_attn_in['w_out'], 'L0_ffn_Wr': _L0_ffn_in['Wr'], 'L0_ffn_Wg': _L0_ffn_in['Wg'], 'L0_ffn_Wu': _L0_ffn_in['Wu'], 'L0_ffn_Wd': _L0_ffn_in['Wd'], 'L0_ffn_Sg': _L0_ffn_in['Sg'], 'L0_ffn_Su': _L0_ffn_in['Su'], 'L0_ffn_Sd': _L0_ffn_in['Sd'], 'L0_ffn_expert_bias': _L0_ffn_in['expert_bias']}
    _x0 = _d['L0_attn_x']
    _d['L0_attn_x'] = jax.random.normal(jax.random.fold_in(jax.random.key(seed), 1), (16, 256, 128), dtype=_x0.dtype)
    del _x0
    return _d

def reference(L0_attn_x, L0_attn_w_qkv, L0_attn_w_out, L0_ffn_Wr, L0_ffn_Wg, L0_ffn_Wu, L0_ffn_Wd, L0_ffn_Sg, L0_ffn_Su, L0_ffn_Sd, L0_ffn_expert_bias):

    def _L0_attn_ref(x, w_qkv, w_out):
        import jax, jax.numpy as jnp
        import numpy as np
        N_FILTERS = 128
        N_HEADS = 16
        b, n, c = x.shape
        h = N_HEADS
        d = c // h
        qkv = jnp.einsum('bnc,ce->bne', x, w_qkv)
        q, k, v = jnp.split(qkv, 3, axis=-1)
        to_heads = lambda t: t.reshape(b, n, h, d).transpose(0, 2, 1, 3)
        q, k, v = (to_heads(q), to_heads(k), to_heads(v))
        scale = jnp.sqrt(jnp.asarray(c, jnp.float32))
        attn = jnp.einsum('bhnd,bhmd->bhnm', q, k) / scale
        attn = jax.nn.softmax(attn, axis=-1)
        out = jnp.einsum('bhnm,bhmd->bhnd', attn, v)
        out = out.transpose(0, 2, 1, 3).reshape(b, n, c)
        return jnp.einsum('bnc,co->bno', out, w_out)

    def _L0_ffn_ref(x, Wr, Wg, Wu, Wd, Sg, Su, Sd, expert_bias):
        import jax, jax.numpy as jnp
        import numpy as np
        B, S, D = (2, 128, 128)
        E, K, F, FS = (8, 2, 64, 128)
        b, s, d = x.shape
        xf = x.reshape(-1, d)
        T = xf.shape[0]
        logits = xf @ Wr + expert_bias
        top_v, top_i = jax.lax.top_k(logits, K)
        probs = jax.nn.softmax(top_v, axis=-1)
        rw = jnp.zeros_like(logits).at[jnp.arange(T)[:, None], top_i].set(probs)
        gate = jnp.einsum('td,edf->tef', xf, Wg)
        up = jnp.einsum('td,edf->tef', xf, Wu)
        h = jax.nn.silu(gate) * up
        eo = jnp.einsum('tef,efd->ted', h, Wd)
        out = jnp.einsum('te,ted->td', rw, eo)
        out = out + jax.nn.silu(xf @ Sg) * (xf @ Su) @ Sd
        return out.reshape(b, s, d)
    x = L0_attn_x
    x = x + _layernorm(_L0_attn_ref(_layernorm(x, axis=-1), L0_attn_w_qkv, L0_attn_w_out), axis=-1)
    x = x + _layernorm(_L0_ffn_ref(_layernorm(x, axis=-1), L0_ffn_Wr, L0_ffn_Wg, L0_ffn_Wu, L0_ffn_Wd, L0_ffn_Sg, L0_ffn_Su, L0_ffn_Sd, L0_ffn_expert_bias), axis=-1)
    return x

_drawn_inputs = setup_inputs


def setup_inputs(seed=0):
    import zlib

    import numpy as np

    out = dict(_drawn_inputs(seed))
    spreads = {'L0_ffn_expert_bias': (0.0, 0.1)}
    factors = {}
    for name, (base, spread) in spreads.items():
        noise = np.random.default_rng([zlib.crc32(name.encode()), seed]).standard_normal(out[name].shape)
        drawn = base * np.exp(spread * noise) if base else spread * noise
        out[name] = jnp.asarray(drawn.astype(out[name].dtype))
    for name, factor in factors.items():
        out[name] = (out[name] * factor).astype(out[name].dtype)
    return out
```

```python
from contextlib import ExitStack

import concourse.bass as bass
from concourse import mybir

F32 = mybir.dt.float32
BF16 = mybir.dt.bfloat16
U32 = mybir.dt.uint32
ALU = mybir.AluOpType
ACT = mybir.ActivationFunctionType
AX = mybir.AxisListType

P = 128
EPS = 1e-5
SLOTS = 16
RING = 3
DMA = 16
PARTS_Q = [(0, 3), (0, 2), (0, 1)]
PARTS_K = [(0, 3), (1, 2), (2, 1)]
ROWS = 48
ROWS_MAX = 51
CHUNKS = 5
ORDER = [4, 0, 1, 2, 3]
LAST_LAG = 5

WHEN = {
    "load_x": (0, 0), "stats1": (0, 2), "aggr1": (0, 3), "rstd1": (0, 2), "apply1": (0, 3), "xT": (0, 4),
    "xT_copy": (0, 4), "qk": (0, 5), "part1": (0, 5), "rest1": (0, 6), "part2": (0, 7),
    "part3": (0, 7), "spill": (0, 8), "stack": (0, 10), "v": (0, 13), "v_copy": (0, 14),
    "maxT": (2, 1), "max1": (2, 1), "max_rest": (2, 2), "max2": (2, 2), "max3": (2, 3),
    "max_spill": (2, 4), "max_stack": (2, 6),
    "pv_copy0": (3, 5), "pv_copy1": (3, 13), "pv_spill0": (3, 6), "pv_spill1": (3, 14),
    "pv_load": (4, 0), "recip": (4, 2), "norm": (4, 3), "proj": (4, 4), "load_x2": (4, 1),
    "stats2": (4, 5), "aggr2": (4, 6), "rstd2": (4, 5), "apply2": (4, 6), "add2": (4, 6),
    "stats3": (4, 7), "aggr3": (4, 8), "rstd3": (4, 7), "apply3": (4, 8), "x3T": (4, 9), "x3T_copy": (4, 9),
    "router": (4, 11), "top": (4, 11), "gate_exp": (4, 12), "gates": (4, 13), "weights": (4, 13),
    "wT": (4, 15), "wT_copy": (5, 0), "w_spill": (5, 0), "w_load": (5, 2),
    "gu0": (4, 10), "gu1": (4, 12), "gu2": (4, 13), "gu3": (4, 14), "gu4": (4, 15),
    "tanh0": (4, 10), "tanh1": (4, 12), "tanh2": (4, 13), "tanh3": (4, 14), "tanh4": (4, 15),
    "h0": (4, 11), "h1": (4, 13), "h2": (4, 14), "h3": (4, 15), "h4": (5, 0),
    "hw0": (5, 3), "hw1": (5, 3), "hw2": (5, 4), "hw3": (5, 4), "down": (5, 7),
    "stats4": (5, 8), "aggr4": (5, 9), "rstd4": (5, 8), "apply4": (5, 9), "add4": (5, 9), "store": (5, 10),
}
S2_SLOT = 8
PV_WHEN = [[(3, 1), (3, 2), (3, 3), (3, 4)], [(3, 9), (3, 10), (3, 11), (3, 12)]]


def head_of(k):
    return 8 * (k % 2) + k // 2


def sandwich(nc, x, w_qkv, w_out, Wr, Wg, Wu, Wd, Sg, Su, Sd, bias, out):
    NB, N, D = x.shape
    E, _, F = Wg.shape
    H = 16
    DH = D // H
    TT = N // P
    SCALE = float(D) ** -0.5
    STEPS = NB + LAST_LAG
    LOOP_FROM = LAST_LAG + 1
    LOOP_TO = LOOP_FROM + RING * ((NB - LOOP_FROM) // RING)
    assert D == P and N == 256 and 2 * F == P and E == 8 and H * DH == D and NB >= LOOP_TO

    with ExitStack() as ctx:
        def sb(name, shape, dt=F32):
            return ctx.enter_context(nc.sbuf_tensor(name, shape, dt))

        def psum(name, shape):
            return ctx.enter_context(nc.psum_tensor(name, shape, F32))

        def sem(name):
            return ctx.enter_context(nc.semaphore(name))

        wqkv_sb = sb("wqkv_sb", [P, 3 * D])
        wqk_sb = sb("wqk_sb", [P, 2, P])
        wout_sb = sb("wout_sb", [P, D])
        wr_sb = sb("wr_sb", [P, E])
        wg_sb = sb("wg_sb", [P, CHUNKS, P])
        wu_sb = sb("wu_sb", [P, CHUNKS, P])
        wd_sb = sb("wd_sb", [P, CHUNKS, D])
        bias_sb = sb("bias_sb", [P, TT, E])
        ident = sb("ident", [P, P])
        iota_i = sb("iota_i", [P, E], mybir.dt.int32)
        iota = sb("iota", [P, E])
        mhalf = sb("mhalf", [P, TT])
        eps = sb("eps", [P, TT])
        x_sb = sb("x_sb", [P, TT, D])
        xn = sb("xn", [P, TT, D])
        xT = sb("xT", [P, N])
        parts = sb("parts", [P, 6, N], BF16)
        rest = sb("rest", [P, 2 * N])
        qs = [sb(f"qs{r}", [P, 8, N], BF16) for r in range(RING)]
        ks = [sb(f"ks{r}", [P, 8, N], BF16) for r in range(RING)]
        va = [sb(f"va{r}", [P, TT, H, 32]) for r in range(RING)]
        mx = sb("mx", [P, TT, H])
        mparts = sb("mparts", [H, 3, N], BF16)
        mrest = sb("mrest", [H, N])
        pr = sb("pr", [P, H, 2 * N])
        pv_sb = sb("pv_sb", [P, 2, N])
        oc = sb("oc", [P, N])
        den = sb("den", [P, N])
        rden = sb("rden", [P, N])
        on = sb("on", [P, N])
        st = {L: sb(f"st{L}", [P, TT, 6]) for L in (1, 2, 3, 4)}
        mv = {L: sb(f"mv{L}", [P, TT, 2]) for L in (1, 2, 3, 4)}
        vareps = {L: sb(f"vareps{L}", [P, TT]) for L in (1, 2, 3, 4)}
        rs = {L: sb(f"rs{L}", [P, TT]) for L in (1, 2, 3, 4)}
        x_res = sb("x_res", [P, TT, D])
        y2 = sb("y2", [P, TT, D])
        x2 = [sb(f"x2_{r}", [P, TT, D]) for r in range(RING)]
        x3 = sb("x3", [P, TT, D])
        x3T = sb("x3T", [P, N])
        y4 = sb("y4", [P, TT, D])
        x4 = sb("x4", [P, TT, D])
        lg = sb("lg", [P, TT, E])
        top_v = sb("top_v", [P, TT, 8])
        top_i = sb("top_i", [P, TT, 8], U32)
        top_f = sb("top_f", [P, TT, 2])
        gd = sb("gd", [P, TT])
        ge = sb("ge", [P, TT])
        g1 = sb("g1", [P, TT])
        gp = sb("gp", [P, 2, TT])
        wa = sb("wa", [P, 2, TT, E])
        rw = sb("rw", [P, TT, E])
        rwT = sb("rwT", [E, N])
        rwb = sb("rwb", [P, 4, N])
        th = sb("th", [P, 2, N])
        ha = sb("ha", [P, 2, N])
        hb = sb("hb", [P, CHUNKS, N])
        hw = sb("hw", [P, 4, N])

        s1p = [psum(f"s1p{n}", [P, TT, N]) for n in range(2)]
        s2p = [psum(f"s2p{n}", [P, TT, N]) for n in range(2)]
        pvp = psum("pvp", [P, 512])
        bank_a = psum("bank_a", [P, 512])
        bank_d = [psum(f"bank_d{n}", [P, 512]) for n in range(2)]

        qk_dram = [nc.dram_tensor(f"qk_dram{r}", [6, 2, DH, 8, N], BF16).ap() for r in range(RING)]
        max_dram = nc.dram_tensor("max_dram", [3, H, N], BF16).ap()
        pv_dram = nc.dram_tensor("pv_dram", [2, P, N], F32).ap()
        rw_dram = nc.dram_tensor("rw_dram", [E, N], F32).ap()

        wqkv_load = sem("wqkv_load")
        w_load = sem("w_load")
        x_load = sem("x_load")
        x_res_load = sem("x_res_load")
        qk_spilled = sem("qk_spilled")
        qk_stacked = sem("qk_stacked")
        max_spilled = sem("max_spilled")
        max_stacked = sem("max_stacked")
        pv_spilled = sem("pv_spilled")
        pv_loaded = sem("pv_loaded")
        rw_spilled = sem("rw_spilled")
        rw_loaded = sem("rw_loaded")
        stored = sem("stored")
        consts = sem("consts")
        ident_zeroed = sem("ident_zeroed")
        iota_i_done = sem("iota_i_done")
        zeroed = sem("zeroed")
        ones_done = sem("ones_done")
        wqk_done = sem("wqk_done")
        ln_x3T = sem("ln_x3T")
        xT_done = sem("xT_done")
        xT_copied = sem("xT_copied")
        qk_done = sem("qk_done")
        part1_done = sem("part1_done")
        rest1_done = sem("rest1_done")
        part2_done = sem("part2_done")
        part3_done = sem("part3_done")
        v_done = sem("v_done")
        v_copied = sem("v_copied")
        s1_done = sem("s1_done")
        max_done = sem("max_done")
        maxT_done = sem("maxT_done")
        max1_done = sem("max1_done")
        max_rest_done = sem("max_rest_done")
        max2_done = sem("max2_done")
        max3_done = sem("max3_done")
        s2_done = sem("s2_done")
        exp_done = sem("exp_done")
        pv_done = sem("pv_done")
        pv_copied = sem("pv_copied")
        recip_done = sem("recip_done")
        norm_done = sem("norm_done")
        proj_done = sem("proj_done")
        add2_done = sem("add2_done")
        x3T_done = sem("x3T_done")
        x3T_copied = sem("x3T_copied")
        router_done = sem("router_done")
        logits_done = sem("logits_done")
        topv_done = sem("topv_done")
        topi_done = sem("topi_done")
        topf_done = sem("topf_done")
        gd_done = sem("gd_done")
        gexp_done = sem("gexp_done")
        g1_done = sem("g1_done")
        gp1_done = sem("gp1_done")
        gp2_done = sem("gp2_done")
        wa_done = sem("wa_done")
        rw_done = sem("rw_done")
        wT_done = sem("wT_done")
        wT_copied = sem("wT_copied")
        gu_done = sem("gu_done")
        tanh_done = sem("tanh_done")
        ha_done = sem("ha_done")
        h_done = sem("h_done")
        hw_done = sem("hw_done")
        down_done = sem("down_done")
        add4_done = sem("add4_done")
        stats_done = {L: sem(f"stats{L}_done") for L in (1, 2, 3, 4)}
        aggr_done = {L: sem(f"aggr{L}_done") for L in (1, 2, 3, 4)}
        vareps_done = {L: sem(f"vareps{L}_done") for L in (1, 2, 3, 4)}
        rstd_done = {L: sem(f"rstd{L}_done") for L in (1, 2, 3, 4)}
        applied = {L: sem(f"applied{L}") for L in (1, 2, 3, 4)}

        block = ctx.enter_context(nc.Block())

        def count(per, b, k=0):
            if isinstance(b, int):
                return per * min(b, NB) + (k if b < NB else 0) if b >= 0 else 0
            return b * per + k if per != 1 else b + k

        def some(n):
            return not isinstance(n, int) or n > 0

        def steps(eng, slots):
            for i in range(LOOP_FROM):
                slots(i, i % RING)
            with eng.Fori(LOOP_FROM, LOOP_TO - RING + 1, RING) as i:
                for r in range(RING):
                    slots(i + r if r else i, (LOOP_FROM + r) % RING)
            for i in range(LOOP_TO, STEPS):
                slots(i, i % RING)

        def live(b):
            return not isinstance(b, int) or 0 <= b < NB

        def due(i, s, name):
            lag, slot = WHEN[name]
            return slot == s and live(i - lag)

        def lag(name):
            return WHEN[name][0]

        @block.sync
        def _(sp):
            sp.dma_start(wqkv_sb[:], w_qkv).then_inc(wqkv_load, DMA)

            def load_weights():
                sp.dma_start(wr_sb[:], Wr).then_inc(w_load, DMA)
                sp.dma_start(wg_sb[:, 4, :], Sg).then_inc(w_load, DMA)
                sp.dma_start(wu_sb[:, 4, :], Su).then_inc(w_load, DMA)
                sp.dma_start(wd_sb[:, 4, :], Sd).then_inc(w_load, DMA)
                for e2 in range(2):
                    es = slice(4 * e2, 4 * e2 + 4)
                    half = slice(F * e2, F * e2 + F)
                    sp.dma_start(wg_sb[:, 0:4, half], Wg[es].rearrange("c d f -> d c f")).then_inc(w_load, DMA)
                    sp.dma_start(wu_sb[:, 0:4, half], Wu[es].rearrange("c d f -> d c f")).then_inc(w_load, DMA)
                    sp.dma_start(wd_sb[half, 0:4, :], Wd[es].rearrange("c f d -> f c d")).then_inc(w_load, DMA)
                for t in range(TT):
                    sp.dma_start(bias_sb[:, t, :], bias.rearrange("(a e) -> a e", a=1).broadcast_to([P, E])).then_inc(w_load, DMA)
                for gj in range(8):
                    for u in range(2):
                        sp.dma_start(wout_sb[16 * gj + 8 * u:16 * gj + 8 * u + 8, :],
                                     w_out[64 * u + 8 * gj:64 * u + 8 * gj + 8, :]).then_inc(w_load, DMA)

            def slots(i, r):
                for s in range(SLOTS):
                    if due(i, s, "load_x"):
                        b = i
                        if some(n_wait := count(TT, b)):
                            sp.wait_ge(applied[1], n_wait)
                        sp.dma_start(x_sb[:], x[b].rearrange("(t p) d -> p t d", p=P)).then_inc(x_load, DMA)
                        if isinstance(i, int) and i == 0:
                            load_weights()
                    if due(i, s, "spill"):
                        b = i
                        sp.wait_ge(part3_done, count(1, b, 1))
                        sp.dma_start(qk_dram[r].rearrange("a u d x n -> (u d x) a n"), parts[:]).then_inc(qk_spilled, DMA)
                    if due(i, s, "stack"):
                        b = i
                        if some(n_wait := count(H, b - 2)):
                            sp.wait_ge(s2_done, n_wait)
                        sp.wait_ge(qk_spilled, count(DMA, b, DMA))
                        for u in range(2):
                            row = 64 * u
                            for n in range(3):
                                first, copies = PARTS_Q[n]
                                src = qk_dram[r][2 * first:2 * (first + copies):2, u].rearrange("a d x n -> a d (x n)")
                                sp.dma_start(qs[r][row:row + 8 * copies], src).then_inc(qk_stacked, DMA)
                                first, copies = PARTS_K[n]
                                src = qk_dram[r][2 * first + 1:2 * first + 2, u].rearrange("a d x n -> a d (x n)").broadcast_to([copies, DH, 8 * N])
                                sp.dma_start(ks[r][row:row + 8 * copies], src).then_inc(qk_stacked, DMA)
                                row += 8 * copies
                    if due(i, s, "max_spill"):
                        b = i - lag("max_spill")
                        sp.wait_ge(max3_done, count(1, b, 1))
                        sp.dma_start(max_dram.rearrange("a h n -> h a n"), mparts[:]).then_inc(max_spilled, DMA)
                    if due(i, s, "max_stack"):
                        b = i - lag("max_stack")
                        sp.wait_ge(max_spilled, count(DMA, b, DMA))
                        q = qs[(r - lag("max_stack")) % RING]
                        for u in range(2):
                            sp.dma_start(q[64 * u + ROWS:64 * u + ROWS_MAX], max_dram[:, 8 * u:8 * u + 8, :]).then_inc(max_stacked, DMA)
                    for g in range(2):
                        if due(i, s, f"pv_spill{g}"):
                            b = i - lag(f"pv_spill{g}")
                            sp.wait_ge(pv_copied, count(2, b, g + 1))
                            sp.dma_start(pv_dram[g], pv_sb[:, g, :]).then_inc(pv_spilled, DMA)
                    if due(i, s, "pv_load"):
                        b = i - lag("pv_load")
                        sp.wait_ge(pv_spilled, count(2 * DMA, b, 2 * DMA))
                        rows = pv_dram.rearrange("g (j k) n -> (g j) k n", k=32)
                        sp.dma_start(oc[:], rows[:, 0:16, :]).then_inc(pv_loaded, DMA)
                        sp.dma_start(den[:], rows[:, 16:32, :]).then_inc(pv_loaded, DMA)
                    if due(i, s, "load_x2"):
                        b = i - lag("load_x2")
                        if some(n_wait := count(1, b)):
                            sp.wait_ge(add2_done, n_wait)
                        sp.dma_start(x_res[:], x[b].rearrange("(t p) d -> p t d", p=P)).then_inc(x_res_load, DMA)
                    if due(i, s, "w_spill"):
                        b = i - lag("w_spill")
                        sp.wait_ge(wT_copied, count(1, b, 1))
                        sp.dma_start(rw_dram, rwT[:]).then_inc(rw_spilled, DMA)
                    if due(i, s, "w_load"):
                        b = i - lag("w_load")
                        sp.wait_ge(rw_spilled, count(DMA, b, DMA))
                        for e2 in range(2):
                            src = rw_dram[4 * e2:4 * e2 + 4].rearrange("(a c) n -> a (c n)", a=1).broadcast_to([F, 4 * N])
                            sp.dma_start(rwb[F * e2:F * e2 + F].rearrange("p c n -> p (c n)"), src).then_inc(rw_loaded, DMA)
                    if due(i, s, "store"):
                        b = i - lag("store")
                        sp.wait_ge(add4_done, count(1, b, 1))
                        sp.dma_start(out[b].rearrange("(t p) d -> p t d", p=P), x4[:]).then_inc(stored, DMA)

            steps(sp, slots)
            sp.wait_ge(stored, DMA * NB)

        @block.tensor
        def _(pe):
            pe.wait_ge(consts, 3)
            pe.wait_ge(wqk_done, 2)

            def s1(b, r, k):
                h = head_of(k)
                row = 64 * (h // 8)
                if k == 0:
                    pe.wait_ge(qk_stacked, count(12 * DMA, b, 12 * DMA))
                    pe.wait_ge(ones_done, 1) if isinstance(b, int) and b == 0 else None
                if some(n_wait := count(H, b, k - 1)):
                    pe.wait_ge(max_done, n_wait)
                for c in range(TT):
                    mm = pe.matmul(s1p[k % 2][:, c, :], qs[r][row:row + ROWS, h % 8, c * P:(c + 1) * P],
                                   ks[r][row:row + ROWS, h % 8, :], start=True, stop=True)
                mm.then_inc(s1_done, 1)

            def s2(b, r, k):
                h = head_of(k)
                row = 64 * (h // 8)
                if k == 0:
                    pe.wait_ge(max_stacked, count(2 * DMA, b, 2 * DMA))
                if some(n_wait := count(H, b, k - 1)):
                    pe.wait_ge(exp_done, n_wait)
                for c in range(TT):
                    mm = pe.matmul(s2p[k % 2][:, c, :], ks[r][row:row + ROWS_MAX, h % 8, c * P:(c + 1) * P],
                                   qs[r][row:row + ROWS_MAX, h % 8, :], start=True, stop=True)
                mm.then_inc(s2_done, 1)

            def pv(b, r, g, n):
                u, c = n // TT, n % TT
                if n == 0:
                    pe.wait_ge(exp_done, count(H, b, 8 * g + 8))
                    pe.wait_ge(v_copied, count(1, b, 1))
                    if some(n_wait := count(2, b, g)):
                        pe.wait_ge(pv_copied, n_wait)
                for j in range(4):
                    k = 8 * g + 2 * j + u
                    mm = pe.matmul(pvp[32 * j:32 * j + 32, 0:N], va[r][:, c, k, :], pr[:, k, c * N:(c + 1) * N],
                                   start=(n == 0), stop=(n == 3))
                if n == 3:
                    mm.then_inc(pv_done, 1)

            def slots(i, r):
                for s in range(SLOTS):
                    if due(i, s, "maxT"):
                        b = i - lag("maxT")
                        pe.wait_ge(max_done, count(H, b, H))
                        pe.wait_ge(v_copied, count(1, b + 1, 1))
                        if some(n_wait := count(1, b - 3, 1)):
                            pe.wait_ge(wT_copied, n_wait)
                        for c in range(TT):
                            mm = pe.transpose(bank_a[0:H, c * P:(c + 1) * P], mx[:, c, :], ident[:])
                        mm.then_inc(maxT_done, 1)
                    if live(i - 1):
                        s1(i - 1, (r - 1) % RING, s)
                    b = i - 2 if s >= S2_SLOT else i - 3
                    if live(b):
                        s2(b, (r - (2 if s >= S2_SLOT else 3)) % RING, (s - S2_SLOT) % SLOTS)
                    for g in range(2):
                        for n in range(4):
                            l, slot = PV_WHEN[g][n]
                            if slot == s and live(i - l):
                                pv(i - l, (r - l) % RING, g, n)
                    if due(i, s, "xT"):
                        b = i
                        pe.wait_ge(applied[1], count(TT, b, TT))
                        if some(n_wait := count(1, b - 2, 1)):
                            pe.wait_ge(max_rest_done, n_wait)
                        if not live(b - 2):
                            if some(n_wait := count(1, b - 1, 1)):
                                pe.wait_ge(v_copied, n_wait)
                        for c in range(TT):
                            mm = pe.transpose(bank_a[:, c * P:(c + 1) * P], xn[:, c, :], ident[:])
                        mm.then_inc(xT_done, 1)
                    if due(i, s, "qk"):
                        pe.wait_ge(xT_copied, count(1, i, 1))
                        for n in range(2):
                            mm = pe.matmul(bank_a[:, n * N:(n + 1) * N], wqk_sb[:, n, :], xT[:], start=True, stop=True)
                        mm.then_inc(qk_done, 1)
                    if due(i, s, "v"):
                        pe.wait_ge(rest1_done, count(1, i, 1))
                        for c in range(TT):
                            mm = pe.matmul(bank_a[:, c * P:(c + 1) * P], xT[:, c * P:(c + 1) * P],
                                           wqkv_sb[:, 2 * D:3 * D].rearrange("p (u x d) -> p x u d", u=2, x=8),
                                           start=True, stop=True)
                        mm.then_inc(v_done, 1)
                    if due(i, s, "proj"):
                        b = i - lag("proj")
                        if isinstance(b, int) and b == 0:
                            pe.wait_ge(w_load, DMA * 28)
                        pe.wait_ge(norm_done, count(1, b, 1))
                        if some(n_wait := count(CHUNKS, b - 1, 4)):
                            pe.wait_ge(h_done, n_wait)
                        for c in range(TT):
                            mm = pe.matmul(bank_d[0][:, c * P:(c + 1) * P], on[:, c * P:(c + 1) * P], wout_sb[:],
                                           start=True, stop=True)
                        mm.then_inc(proj_done, 1)
                    if due(i, s, "x3T"):
                        b = i - lag("x3T")
                        pe.wait_ge(applied[3], count(TT, b, TT))
                        if some(n_wait := count(CHUNKS, b)):
                            pe.wait_ge(h_done, n_wait)
                        for c in range(TT):
                            mm = pe.transpose(bank_d[1][:, c * P:(c + 1) * P], x3[:, c, :], ident[:])
                        mm.then_inc(x3T_done, 1)
                    if due(i, s, "router"):
                        b = i - lag("router")
                        pe.wait_ge(x3T_copied, count(1, b, 1))
                        if some(n_wait := count(TT, b)):
                            pe.wait_ge(applied[4], n_wait)
                        for c in range(TT):
                            mm = pe.matmul(bank_d[0][:, c * E:(c + 1) * E], x3T[:, c * P:(c + 1) * P], wr_sb[:],
                                           start=True, stop=True)
                        mm.then_inc(router_done, 1)
                    for n in range(CHUNKS):
                        if due(i, s, f"gu{n}"):
                            b = i - lag(f"gu{n}")
                            c = ORDER[n]
                            if n == 0:
                                pe.wait_ge(x3T_copied, count(1, b, 1))
                            elif n == 1:
                                pe.wait_ge(logits_done, count(1, b, 1))
                            else:
                                if some(n_wait := count(CHUNKS, b, n - 1)):
                                    pe.wait_ge(h_done, n_wait)
                            bank = bank_d[(n + 1) % 2]
                            pe.matmul(bank[:, 0:N], wg_sb[:, c, :], x3T[:], start=True, stop=True)
                            pe.matmul(bank[:, N:2 * N], wu_sb[:, c, :], x3T[:], start=True, stop=True).then_inc(gu_done, 1)
                    if due(i, s, "wT"):
                        b = i - lag("wT")
                        pe.wait_ge(rw_done, count(1, b, 1))
                        pe.wait_ge(v_copied, count(1, b + 4, 1))
                        for c in range(TT):
                            mm = pe.transpose(bank_a[0:E, c * P:(c + 1) * P], rw[:, c, :], ident[:])
                        mm.then_inc(wT_done, 1)
                    if due(i, s, "down"):
                        b = i - lag("down")
                        pe.wait_ge(hw_done, count(4, b, 4))
                        pe.wait_ge(h_done, count(CHUNKS, b, CHUNKS))
                        pe.wait_ge(applied[2], count(TT, b + 1, TT))
                        for c in range(TT):
                            for n in range(CHUNKS):
                                src = hw[:, n, c * P:(c + 1) * P] if n < 4 else hb[:, 4, c * P:(c + 1) * P]
                                mm = pe.matmul(bank_d[0][:, c * P:(c + 1) * P], src, wd_sb[:, n, :],
                                               start=(n == 0), stop=(n == CHUNKS - 1))
                        mm.then_inc(down_done, 1)

            steps(pe, slots)

        @block.scalar
        def _(act):
            def slots(i, r):
                for s in range(SLOTS):
                    b = i - 2 if s >= S2_SLOT else i - 3
                    if live(b):
                        k = (s - S2_SLOT) % SLOTS
                        act.wait_ge(s2_done, count(H, b, k + 1))
                        if some(n_wait := count(2, b - 1, k // 8 + 1)):
                            act.wait_ge(pv_done, n_wait)
                        nc.scalar.activation(pr[:, k, :], s2p[k % 2][:].rearrange("p c n -> p (c n)"),
                                             ACT.Exp, scale=SCALE).then_inc(exp_done, 1)
                    if due(i, s, "max1"):
                        b = i - lag("max1")
                        act.wait_ge(maxT_done, count(1, b, 1))
                        if some(n_wait := count(DMA, b)):
                            act.wait_ge(max_spilled, n_wait)
                        nc.scalar.activation(mparts[:, 0, :], bank_a[0:H, 0:N], ACT.Copy, scale=-1.0).then_inc(max1_done, 1)
                    if due(i, s, "max2"):
                        b = i - lag("max2")
                        act.wait_ge(max_rest_done, count(1, b, 1))
                        if some(n_wait := count(DMA, b)):
                            act.wait_ge(max_spilled, n_wait)
                        nc.scalar.copy(mparts[:, 1, :], mrest[:]).then_inc(max2_done, 1)
                    if due(i, s, "xT_copy"):
                        act.wait_ge(xT_done, count(1, i, 1))
                        if some(n_wait := count(1, i)):
                            act.wait_ge(v_done, n_wait)
                        nc.scalar.copy(xT[:], bank_a[:, 0:N]).then_inc(xT_copied, 1)
                    if due(i, s, "part1"):
                        act.wait_ge(qk_done, count(1, i, 1))
                        if some(n_wait := count(DMA, i)):
                            act.wait_ge(qk_spilled, n_wait)
                        nc.scalar.copy(parts[:, 0:2, :].rearrange("p a n -> p (a n)"), bank_a[:]).then_inc(part1_done, 1)
                    if due(i, s, "part2"):
                        act.wait_ge(rest1_done, count(1, i, 1))
                        nc.scalar.copy(parts[:, 2:4, :].rearrange("p a n -> p (a n)"), rest[:]).then_inc(part2_done, 1)
                    if due(i, s, "v_copy"):
                        b = i
                        act.wait_ge(v_done, count(1, b, 1))
                        if some(n_wait := count(2, b - 2)):
                            act.wait_ge(pv_done, n_wait)
                        dst = va[r][:].rearrange("p c (x u) k -> p (c x) (u k)", u=2)
                        for u in range(2):
                            cp = nc.scalar.copy(dst[:, :, 40 * u:40 * u + DH],
                                                bank_a[:, 0:N].rearrange("p (x u d) -> p x u d", u=2, d=DH)[:, :, u, :])
                        cp.then_inc(v_copied, 1)
                    for g in range(2):
                        if due(i, s, f"pv_copy{g}"):
                            b = i - lag(f"pv_copy{g}")
                            act.wait_ge(pv_done, count(2, b, g + 1))
                            if some(n_wait := count(2 * DMA, b - 1, DMA * (g + 1))):
                                act.wait_ge(pv_spilled, n_wait)
                            nc.scalar.copy(pv_sb[:, g, :], pvp[:, 0:N]).then_inc(pv_copied, 1)
                    if due(i, s, "x3T_copy"):
                        b = i - lag("x3T_copy")
                        act.wait_ge(x3T_done, count(1, b, 1))
                        if some(n_wait := count(CHUNKS, b)):
                            act.wait_ge(gu_done, n_wait)
                        nc.scalar.copy(x3T[:], bank_d[1][:, 0:N]).then_inc(x3T_copied, 1)
                    for n in range(CHUNKS):
                        if due(i, s, f"tanh{n}"):
                            b = i - lag(f"tanh{n}")
                            act.wait_ge(gu_done, count(CHUNKS, b, n + 1))
                            if some(n_wait := count(CHUNKS, b, n - 1)):
                                act.wait_ge(ha_done, n_wait)
                            nc.scalar.activation(th[:, n % 2, :], bank_d[(n + 1) % 2][:, 0:N], ACT.Tanh, scale=0.5).then_inc(tanh_done, 1)
                    if due(i, s, "gate_exp"):
                        b = i - lag("gate_exp")
                        act.wait_ge(gd_done, count(1, b, 1))
                        if some(n_wait := count(1, b)):
                            act.wait_ge(gp2_done, n_wait)
                        nc.scalar.activation(ge[:], gd[:], ACT.Exp).then_inc(gexp_done, 1)
                    if due(i, s, "wT_copy"):
                        b = i - lag("wT_copy")
                        act.wait_ge(wT_done, count(1, b, 1))
                        if some(n_wait := count(DMA, b)):
                            act.wait_ge(rw_spilled, n_wait)
                        nc.scalar.copy(rwT[:], bank_a[0:E, 0:N]).then_inc(wT_copied, 1)

            steps(act, slots)

        @block.vector
        def _(dve):
            for r in range(RING):
                nc.vector.memset(ks[r][:], 1.0)
            nc.vector.memset(eps[:], EPS)
            nc.vector.memset(mhalf[:], -0.5).then_inc(consts, 1)
            for r in range(RING):
                nc.vector.memset(va[r][:], 0.0).then_inc(zeroed, 1)
            dve.wait_ge(zeroed, RING)
            for r in range(RING):
                dst = va[r][:].rearrange("p c (x u) k -> p (c x) (u k)", u=2)
                for u in range(2):
                    one = nc.vector.memset(dst[:, :, 40 * u + 16:40 * u + 24], 1.0)
            one.then_inc(ones_done, 1)
            dve.wait_ge(wqkv_load, DMA)
            for n in range(2):
                nc.vector.tensor_copy(wqk_sb[:, n, :].rearrange("p (u d x) -> p u d x", u=2, d=DH),
                                      wqkv_sb[:, n * D:(n + 1) * D].rearrange("p (u x d) -> p u d x", u=2, x=8)).then_inc(wqk_done, 1)
            dve.wait_ge(iota_i_done, 1)
            nc.vector.tensor_copy(iota[:], iota_i[:]).then_inc(consts, 1)

            def stats(L, b, tiles):
                if some(n_wait := count(TT, b)):
                    dve.wait_ge(aggr_done[L], n_wait)
                for t in range(TT):
                    nc.vector.bn_stats(st[L][:, t, :], tiles(t)).then_inc(stats_done[L], 1)

            def apply(L, b, dst, tiles):
                dve.wait_ge(rstd_done[L], count(1, b, 1))
                for t in range(TT):
                    nc.vector.tensor_scalar(dst[:, t, :], tiles(t), mv[L][:, t, 0:1], rs[L][:, t:t + 1],
                                            ALU.subtract, ALU.mult).then_inc(applied[L], 1)

            def half(bank):
                return lambda t: bank[:, t * P:(t + 1) * P]

            def slots(i, r):
                for s in range(SLOTS):
                    if due(i, s, "max_rest"):
                        b = i - lag("max_rest")
                        dve.wait_ge(max1_done, count(1, b, 1))
                        if some(n_wait := count(1, b)):
                            dve.wait_ge(max3_done, n_wait)
                        nc.vector.scalar_tensor_tensor(out=mrest[:], in0=bank_a[0:H, 0:N], scalar=-1.0, in1=mparts[:, 0, :],
                                                       op0=ALU.mult, op1=ALU.subtract).then_inc(max_rest_done, 1)
                    for L in (1, 2, 3, 4):
                        if due(i, s, f"aggr{L}"):
                            b = i - lag(f"aggr{L}")
                            dve.wait_ge(stats_done[L], count(TT, b, TT))
                            if some(n_wait := count(TT, b)):
                                dve.wait_ge(applied[L], n_wait)
                    if live(i - 1):
                        b = i - 1
                        dve.wait_ge(s1_done, count(H, b, s + 1))
                        if s == 0:
                            if some(n_wait := count(1, b)):
                                dve.wait_ge(maxT_done, n_wait)
                        nc.vector.tensor_reduce(mx[:, :, head_of(s)], s1p[s % 2][:], AX.X, ALU.max).then_inc(max_done, 1)
                    for L in (1, 2, 3, 4):
                        if due(i, s, f"aggr{L}"):
                            for t in range(TT):
                                nc.vector.bn_aggr(mv[L][:, t, :], st[L][:, t, :]).then_inc(aggr_done[L], 1)
                    if due(i, s, "stats1"):
                        dve.wait_ge(x_load, count(DMA, i, DMA))
                        stats(1, i, lambda t: x_sb[:, t, :])
                    if due(i, s, "apply1"):
                        if some(n_wait := count(1, i)):
                            dve.wait_ge(xT_done, n_wait)
                        apply(1, i, xn, lambda t: x_sb[:, t, :])
                    if due(i, s, "rest1"):
                        b = i
                        dve.wait_ge(part1_done, count(1, b, 1))
                        if some(n_wait := count(1, b)):
                            dve.wait_ge(part3_done, n_wait)
                        nc.vector.tensor_tensor(rest[:], bank_a[:], parts[:, 0:2, :].rearrange("p a n -> p (a n)"),
                                                ALU.subtract).then_inc(rest1_done, 1)
                    if due(i, s, "recip"):
                        b = i - lag("recip")
                        dve.wait_ge(pv_loaded, count(2 * DMA, b, 2 * DMA))
                        if some(n_wait := count(1, b)):
                            dve.wait_ge(norm_done, n_wait)
                        nc.vector.reciprocal(rden[:], den[:]).then_inc(recip_done, 1)
                    if due(i, s, "stats2"):
                        b = i - lag("stats2")
                        dve.wait_ge(proj_done, count(1, b, 1))
                        stats(2, b, half(bank_d[0]))
                    if due(i, s, "apply2"):
                        b = i - lag("apply2")
                        if some(n_wait := count(1, b)):
                            dve.wait_ge(add2_done, n_wait)
                        apply(2, b, y2, half(bank_d[0]))
                    if due(i, s, "stats3"):
                        b = i - lag("stats3")
                        x2b = x2[(r - lag("stats3")) % RING]
                        dve.wait_ge(add2_done, count(1, b, 1))
                        stats(3, b, lambda t: x2b[:, t, :])
                    if due(i, s, "apply3"):
                        b = i - lag("apply3")
                        x2b = x2[(r - lag("apply3")) % RING]
                        if some(n_wait := count(1, b)):
                            dve.wait_ge(x3T_done, n_wait)
                        apply(3, b, x3, lambda t: x2b[:, t, :])
                    if due(i, s, "top"):
                        b = i - lag("top")
                        dve.wait_ge(router_done, count(1, b, 1))
                        if some(n_wait := count(TT, b)):
                            dve.wait_ge(topi_done, n_wait)
                        nc.vector.tensor_tensor(lg[:].rearrange("p t e -> p (t e)"), bank_d[0][:, 0:TT * E],
                                                bias_sb[:].rearrange("p t e -> p (t e)"), ALU.add).then_inc(logits_done, 1)
                        dve.wait_ge(consts, 3)
                        dve.wait_ge(logits_done, count(1, b, 1))
                        if some(n_wait := count(1, b)):
                            dve.wait_ge(gd_done, n_wait)
                        for t in range(TT):
                            nc.vector.max(top_v[:, t, :], lg[:, t, :]).then_inc(topv_done, 1)
                        dve.wait_ge(topv_done, count(TT, b, TT))
                        if some(n_wait := count(1, b)):
                            dve.wait_ge(gexp_done, n_wait)
                        nc.vector.tensor_tensor(gd[:], top_v[:, :, 1], top_v[:, :, 0], ALU.subtract).then_inc(gd_done, 1)
                        dve.wait_ge(consts, 3)
                        if some(n_wait := count(1, b)):
                            dve.wait_ge(topf_done, n_wait)
                        for t in range(TT):
                            nc.vector.max_index(top_i[:, t, :], top_v[:, t, :], lg[:, t, :]).then_inc(topi_done, 1)
                        dve.wait_ge(topi_done, count(TT, b, TT))
                        if some(n_wait := count(2 * TT, b)):
                            dve.wait_ge(wa_done, n_wait)
                        nc.vector.tensor_copy(top_f[:], top_i[:, :, 0:2]).then_inc(topf_done, 1)
                    if due(i, s, "gates"):
                        b = i - lag("gates")
                        dve.wait_ge(gexp_done, count(1, b, 1))
                        if some(n_wait := count(1, b)):
                            dve.wait_ge(gp1_done, n_wait)
                        nc.vector.tensor_scalar(g1[:], ge[:], 1.0, None, ALU.add).then_inc(g1_done, 1)
                        dve.wait_ge(g1_done, count(1, b, 1))
                        if some(n_wait := count(2 * TT, b)):
                            dve.wait_ge(wa_done, n_wait)
                        nc.vector.reciprocal(gp[:, 0, :], g1[:]).then_inc(gp1_done, 1)
                        dve.wait_ge(gp1_done, count(1, b, 1))
                        nc.vector.tensor_tensor(gp[:, 1, :], gp[:, 0, :], ge[:], ALU.mult).then_inc(gp2_done, 1)
                        dve.wait_ge(gp2_done, count(1, b, 1))
                        dve.wait_ge(topf_done, count(1, b, 1))
                        if some(n_wait := count(1, b)):
                            dve.wait_ge(rw_done, n_wait)
                        for a in range(2):
                            for t in range(TT):
                                nc.vector.tensor_scalar(wa[:, a, t, :], iota[:], top_f[:, t, a:a + 1], gp[:, a, t:t + 1],
                                                        ALU.is_equal, ALU.mult).then_inc(wa_done, 1)
                    for n in range(CHUNKS):
                        if due(i, s, f"h{n}"):
                            b = i - lag(f"h{n}")
                            bank = bank_d[(n + 1) % 2]
                            dve.wait_ge(tanh_done, count(CHUNKS, b, n + 1))
                            if some(n_wait := count(CHUNKS, b, n - 1)):
                                dve.wait_ge(h_done, n_wait)
                            nc.vector.scalar_tensor_tensor(out=ha[:, n % 2, :], in0=th[:, n % 2, :], scalar=1.0, in1=bank[:, 0:N],
                                                           op0=ALU.add, op1=ALU.mult).then_inc(ha_done, 1)
                            dve.wait_ge(ha_done, count(CHUNKS, b, n + 1))
                            if some(n_wait := count(1, b)):
                                dve.wait_ge(down_done, n_wait)
                            nc.vector.scalar_tensor_tensor(out=hb[:, ORDER[n], :], in0=ha[:, n % 2, :], scalar=0.5, in1=bank[:, N:2 * N],
                                                           op0=ALU.mult, op1=ALU.mult).then_inc(h_done, 1)
                    if due(i, s, "stats4"):
                        b = i - lag("stats4")
                        dve.wait_ge(down_done, count(1, b, 1))
                        stats(4, b, half(bank_d[0]))
                    if due(i, s, "apply4"):
                        b = i - lag("apply4")
                        if some(n_wait := count(1, b)):
                            dve.wait_ge(add4_done, n_wait)
                        apply(4, b, y4, half(bank_d[0]))

            steps(dve, slots)

        @block.gpsimd
        def _(pool):
            nc.gpsimd.memset(ident[:], 0.0).then_inc(ident_zeroed, 1)
            pool.wait_ge(ident_zeroed, 1)
            nc.gpsimd.affine_select(out=ident[:], in_=ident[:], compare_op=ALU.not_equal, fill=1.0, base=0,
                                    pattern=[[-1, P]], channel_multiplier=1).then_inc(consts, 1)
            nc.gpsimd.iota(iota_i[:], pattern=[[1, E]], base=0, channel_multiplier=0).then_inc(iota_i_done, 1)
            pool.wait_ge(consts, 3)

            def rstd(L, b):
                pool.wait_ge(aggr_done[L], count(TT, b, TT))
                if some(n_wait := count(1, b)):
                    pool.wait_ge(rstd_done[L], n_wait)
                nc.gpsimd.tensor_tensor(vareps[L][:], mv[L][:, :, 1], eps[:], ALU.add).then_inc(vareps_done[L], 1)
                pool.wait_ge(vareps_done[L], count(1, b, 1))
                if some(n_wait := count(TT, b)):
                    pool.wait_ge(applied[L], n_wait)
                nc.gpsimd.tensor_tensor(rs[L][:], vareps[L][:], mhalf[:], ALU.pow).then_inc(rstd_done[L], 1)

            def flat(tile):
                return tile[:].rearrange("p t d -> p (t d)")

            def slots(i, r):
                for s in range(SLOTS):
                    for L in (1, 2, 3, 4):
                        if due(i, s, f"rstd{L}"):
                            rstd(L, i - lag(f"rstd{L}"))
                    if due(i, s, "max3"):
                        b = i - lag("max3")
                        pool.wait_ge(max2_done, count(1, b, 1))
                        if some(n_wait := count(DMA, b)):
                            pool.wait_ge(max_spilled, n_wait)
                        nc.gpsimd.tensor_tensor(mparts[:, 2, :], mrest[:], mparts[:, 1, :], ALU.subtract).then_inc(max3_done, 1)
                    if due(i, s, "part3"):
                        b = i
                        pool.wait_ge(part2_done, count(1, b, 1))
                        if some(n_wait := count(DMA, b)):
                            pool.wait_ge(qk_spilled, n_wait)
                        nc.gpsimd.tensor_tensor(parts[:, 4:6, :].rearrange("p a n -> p (a n)"), rest[:],
                                                parts[:, 2:4, :].rearrange("p a n -> p (a n)"), ALU.subtract).then_inc(part3_done, 1)
                    if due(i, s, "norm"):
                        b = i - lag("norm")
                        pool.wait_ge(recip_done, count(1, b, 1))
                        if some(n_wait := count(1, b)):
                            pool.wait_ge(proj_done, n_wait)
                        nc.gpsimd.tensor_tensor(on[:], oc[:], rden[:], ALU.mult).then_inc(norm_done, 1)
                    if due(i, s, "add2"):
                        b = i - lag("add2")
                        pool.wait_ge(applied[2], count(TT, b, TT))
                        pool.wait_ge(x_res_load, count(DMA, b, DMA))
                        if some(n_wait := count(1, b - 2)):
                            pool.wait_ge(add4_done, n_wait)
                        nc.gpsimd.tensor_tensor(flat(x2[(r - lag("add2")) % RING]), flat(y2), flat(x_res), ALU.add).then_inc(add2_done, 1)
                    if due(i, s, "weights"):
                        b = i - lag("weights")
                        pool.wait_ge(wa_done, count(2 * TT, b, 2 * TT))
                        if some(n_wait := count(1, b)):
                            pool.wait_ge(wT_done, n_wait)
                        nc.gpsimd.tensor_tensor(flat(rw), wa[:, 0].rearrange("p t e -> p (t e)"),
                                                wa[:, 1].rearrange("p t e -> p (t e)"), ALU.add).then_inc(rw_done, 1)
                    for n in range(4):
                        if due(i, s, f"hw{n}"):
                            b = i - lag(f"hw{n}")
                            if n == 0:
                                pool.wait_ge(rw_loaded, count(2 * DMA, b, 2 * DMA))
                                if some(n_wait := count(1, b)):
                                    pool.wait_ge(down_done, n_wait)
                            pool.wait_ge(h_done, count(CHUNKS, b, n + 2))
                            nc.gpsimd.tensor_tensor(hw[:, n, :], hb[:, n, :], rwb[:, n, :], ALU.mult).then_inc(hw_done, 1)
                    if due(i, s, "add4"):
                        b = i - lag("add4")
                        pool.wait_ge(applied[4], count(TT, b, TT))
                        if some(n_wait := count(DMA, b)):
                            pool.wait_ge(stored, n_wait)
                        nc.gpsimd.tensor_tensor(flat(x4), flat(y4), flat(x2[(r - lag("add4")) % RING]), ALU.add).then_inc(add4_done, 1)

            steps(pool, slots)


_INS = ["L0_attn_x", "L0_attn_w_qkv", "L0_attn_w_out", "L0_ffn_Wr", "L0_ffn_Wg", "L0_ffn_Wu", "L0_ffn_Wd",
        "L0_ffn_Sg", "L0_ffn_Su", "L0_ffn_Sd", "L0_ffn_expert_bias"]


def kernel(**inputs):
    import numpy as _np
    import concourse.bacc as _bacc
    from concourse import mybir as _mybir
    from concourse.bass_utils import run_bass_kernel_spmd as _run

    nc = _bacc.Bacc("TRN2", target_bir_lowering=False, num_devices=1)
    arrays, args = {}, []
    for name in _INS:
        a = _np.ascontiguousarray(inputs[name])
        arrays[f"in_{name}_dram"] = a
        args.append(nc.dram_tensor(f"in_{name}_dram", a.shape, _mybir.dt.from_np(a.dtype), kind="ExternalInput").ap())
    shape = inputs["L0_attn_x"].shape
    args.append(nc.dram_tensor("out_0_dram", shape, _mybir.dt.float32, kind="ExternalOutput").ap())
    sandwich(nc, *args)
    r = _run(nc, [arrays], core_ids=[0])
    return r.results[0]["out_0_dram"]
```

```python
from contextlib import ExitStack

import concourse.bass as bass
from concourse import mybir

F32 = mybir.dt.float32
BF16 = mybir.dt.bfloat16
U32 = mybir.dt.uint32
ALU = mybir.AluOpType
ACT = mybir.ActivationFunctionType
AX = mybir.AxisListType

P = 128
EPS = 1e-5
SLOTS = 16
RING = 3
DMA = 16
PARTS_Q = [(0, 3), (0, 2), (0, 1)]
PARTS_K = [(0, 3), (1, 2), (2, 1)]
ROWS = 48
ROWS_MAX = 51
CHUNKS = 5
ORDER = [4, 0, 1, 2, 3]

AT = {
    "load_x": 0, "stats1": 2, "aggr1": 3, "rstd1": 3, "apply1": 6, "xT": 6, "xT_copy": 6,
    "qk": 7, "part1": 8, "rest1": 9, "part2": 10, "part3": 11, "spill": 11, "stack": 19,
    "v": 26, "v_copy": 27,
    "s1": 27, "maxT": 45, "max1": 45, "max_rest": 45, "max2": 45, "max3": 46,
    "max_spill": 46, "max_stack": 48,
    "s2": 51, "pv0": 59, "pv_copy0": 63, "pv_spill0": 64, "pv1": 67, "pv_copy1": 71,
    "pv_spill1": 72, "pv_load": 74, "recip": 76, "load_x2": 77, "norm": 78,
    "proj": 80, "proj_copy": 81, "stats2": 82, "aggr2": 83, "rstd2": 84, "apply2": 85, "add2": 85,
    "stats3": 87, "aggr3": 88, "rstd3": 86, "apply3": 90, "x3T": 92, "x3T_copy": 92,
    "router": 93, "top": 94, "gate_exp": 95, "gates": 96, "weights": 97, "wT": 98, "wT_copy": 99,
    "w_spill": 100, "w_load": 102,
    "gu0": 97, "gu1": 98, "gu2": 100, "gu3": 102, "gu4": 105,
    "tanh0": 97, "tanh1": 99, "tanh2": 102, "tanh3": 103, "tanh4": 106,
    "h0": 99, "h1": 100, "h2": 102, "h3": 105, "h4": 107,
    "hw0": 106, "hw1": 106, "hw2": 107, "hw3": 109, "down0": 110, "down1": 111, "down_copy": 112,
    "stats4": 113, "aggr4": 114, "rstd4": 114, "apply4": 115, "add4": 116, "store": 117,
}
PV_EVERY = 1
STACK_EVERY = 1
WHEN = {name: divmod(at, SLOTS) for name, at in AT.items()}
LAST_LAG = max(AT.values()) // SLOTS
BANK = [1, 0, 1, 0, 1]


def head_of(k):
    return 8 * (k % 2) + k // 2


def sandwich(nc, x, w_qkv, w_out, Wr, Wg, Wu, Wd, Sg, Su, Sd, bias, out):
    NB, N, D = x.shape
    E, _, F = Wg.shape
    H = 16
    DH = D // H
    TT = N // P
    SCALE = float(D) ** -0.5
    STEPS = NB + LAST_LAG
    LOOP_FROM = LAST_LAG + 1
    LOOP_TO = LOOP_FROM + RING * ((NB - LOOP_FROM) // RING)
    assert D == P and N == 256 and 2 * F == P and E == 8 and H * DH == D and NB >= LOOP_TO

    with ExitStack() as ctx:
        def sb(name, shape, dt=F32):
            return ctx.enter_context(nc.sbuf_tensor(name, shape, dt))

        def psum(name, shape):
            return ctx.enter_context(nc.psum_tensor(name, shape, F32))

        def sem(name):
            return ctx.enter_context(nc.semaphore(name))

        wqkv_sb = sb("wqkv_sb", [P, 3 * D])
        wqk_sb = sb("wqk_sb", [P, 2, P])
        wout_sb = sb("wout_sb", [P, D])
        wr_sb = sb("wr_sb", [P, E])
        wg_sb = sb("wg_sb", [P, CHUNKS, P])
        wu_sb = sb("wu_sb", [P, CHUNKS, P])
        wd_sb = sb("wd_sb", [P, CHUNKS, D])
        bias_sb = sb("bias_sb", [P, TT, E])
        ident = sb("ident", [P, P])
        iota_i = sb("iota_i", [P, E], mybir.dt.int32)
        iota = sb("iota", [P, E])
        mhalf = sb("mhalf", [P, TT])
        eps = sb("eps", [P, TT])
        x_sb = sb("x_sb", [P, TT, D])
        xn = sb("xn", [P, TT, D])
        xT = [sb(f"xT{r}", [P, N]) for r in range(RING)]
        parts = sb("parts", [P, 6, N], BF16)
        rest = sb("rest", [P, 2 * N])
        qs = [sb(f"qs{r}", [P, 8, N], BF16) for r in range(RING)]
        ks = [sb(f"ks{r}", [P, 8, N], BF16) for r in range(RING)]
        va = [sb(f"va{r}", [P, TT, H, 32]) for r in range(RING)]
        mx = [sb(f"mx{r}", [P, TT, H]) for r in range(RING)]
        mparts = sb("mparts", [H, 3, N], BF16)
        mrest = sb("mrest", [H, N])
        pr = sb("pr", [P, H, 2 * N])
        pv_sb = sb("pv_sb", [P, 2, N])
        oc = sb("oc", [P, N])
        den = sb("den", [P, N])
        rden = sb("rden", [P, N])
        on = sb("on", [P, N])
        st = {L: sb(f"st{L}", [P, TT, 6]) for L in (1, 2, 3, 4)}
        mv = {L: sb(f"mv{L}", [P, TT, 2]) for L in (1, 2, 3, 4)}
        vareps = {L: sb(f"vareps{L}", [P, TT]) for L in (1, 2, 3, 4)}
        rs = {L: sb(f"rs{L}", [P, TT]) for L in (1, 2, 3, 4)}
        x_res = sb("x_res", [P, TT, D])
        proj = sb("proj", [P, TT, D])
        y2 = sb("y2", [P, TT, D])
        x2 = [sb(f"x2_{r}", [P, TT, D]) for r in range(RING)]
        x3 = sb("x3", [P, TT, D])
        x3T = sb("x3T", [P, N])
        down = sb("down", [P, TT, D])
        y4 = sb("y4", [P, TT, D])
        x4 = sb("x4", [P, TT, D])
        lg = sb("lg", [P, TT, E])
        top_v = sb("top_v", [P, TT, 8])
        top_i = sb("top_i", [P, TT, 8], U32)
        top_f = sb("top_f", [P, TT, 2])
        gd = sb("gd", [P, TT])
        ge = sb("ge", [P, TT])
        g1 = sb("g1", [P, TT])
        gp = sb("gp", [P, 2, TT])
        wa = sb("wa", [P, 2, TT, E])
        rw = sb("rw", [P, TT, E])
        rwT = sb("rwT", [E, N])
        rwb = sb("rwb", [P, 4, N])
        th = sb("th", [P, 2, N])
        ha = sb("ha", [P, 2, N])
        hb = sb("hb", [P, CHUNKS, N])
        hw = sb("hw", [P, 4, N])

        s1p = [psum(f"s1p{n}", [P, TT, N]) for n in range(2)]
        s2p = [psum(f"s2p{n}", [P, TT, N]) for n in range(2)]
        pvp = psum("pvp", [P, 512])
        bank_a = psum("bank_a", [P, 512])
        bank_d = [psum(f"bank_d{n}", [P, 512]) for n in range(2)]

        qk_dram = [nc.dram_tensor(f"qk_dram{r}", [6, 2, DH, 8, N], BF16).ap() for r in range(RING)]
        max_dram = nc.dram_tensor("max_dram", [3, H, N], BF16).ap()
        pv_dram = nc.dram_tensor("pv_dram", [2, P, N], F32).ap()
        rw_dram = nc.dram_tensor("rw_dram", [E, N], F32).ap()

        wqkv_load = sem("wqkv_load")
        w_load = sem("w_load")
        x_load = sem("x_load")
        x_res_load = sem("x_res_load")
        qk_spilled = sem("qk_spilled")
        qk_stacked = sem("qk_stacked")
        max_spilled = sem("max_spilled")
        max_stacked = sem("max_stacked")
        pv_spilled = sem("pv_spilled")
        pv_loaded = sem("pv_loaded")
        rw_spilled = sem("rw_spilled")
        rw_loaded = sem("rw_loaded")
        stored = sem("stored")
        consts = sem("consts")
        ident_zeroed = sem("ident_zeroed")
        iota_i_done = sem("iota_i_done")
        zeroed = sem("zeroed")
        ones_done = sem("ones_done")
        wqk_done = sem("wqk_done")
        xT_done = sem("xT_done")
        xT_copied = sem("xT_copied")
        qk_done = sem("qk_done")
        part1_done = sem("part1_done")
        rest1_done = sem("rest1_done")
        part2_done = sem("part2_done")
        part3_done = sem("part3_done")
        v_done = sem("v_done")
        v_copied = sem("v_copied")
        s1_done = sem("s1_done")
        max_done = sem("max_done")
        maxT_done = sem("maxT_done")
        max1_done = sem("max1_done")
        max_rest_done = sem("max_rest_done")
        max2_done = sem("max2_done")
        max3_done = sem("max3_done")
        s2_done = sem("s2_done")
        exp_done = sem("exp_done")
        pv_done = sem("pv_done")
        pv_copied = sem("pv_copied")
        recip_done = sem("recip_done")
        norm_done = sem("norm_done")
        proj_done = sem("proj_done")
        proj_copied = sem("proj_copied")
        add2_done = sem("add2_done")
        x3T_done = sem("x3T_done")
        x3T_copied = sem("x3T_copied")
        router_done = sem("router_done")
        logits_done = sem("logits_done")
        topv_done = sem("topv_done")
        topi_done = sem("topi_done")
        topf_done = sem("topf_done")
        gd_done = sem("gd_done")
        gexp_done = sem("gexp_done")
        g1_done = sem("g1_done")
        gp1_done = sem("gp1_done")
        gp2_done = sem("gp2_done")
        wa_done = sem("wa_done")
        rw_done = sem("rw_done")
        wT_done = sem("wT_done")
        wT_copied = sem("wT_copied")
        gu_done = sem("gu_done")
        tanh_done = sem("tanh_done")
        ha_done = sem("ha_done")
        h_done = sem("h_done")
        hw_done = sem("hw_done")
        down_done = sem("down_done")
        down_copied = sem("down_copied")
        add4_done = sem("add4_done")
        stats_done = {L: sem(f"stats{L}_done") for L in (1, 2, 3, 4)}
        aggr_done = {L: sem(f"aggr{L}_done") for L in (1, 2, 3, 4)}
        vareps_done = {L: sem(f"vareps{L}_done") for L in (1, 2, 3, 4)}
        rstd_done = {L: sem(f"rstd{L}_done") for L in (1, 2, 3, 4)}
        applied = {L: sem(f"applied{L}") for L in (1, 2, 3, 4)}

        block = ctx.enter_context(nc.Block())

        def count(per, b, k=0):
            if isinstance(b, int):
                return per * min(b, NB) + (k if b < NB else 0) if b >= 0 else 0
            return b * per + k if per != 1 else b + k

        def some(n):
            return not isinstance(n, int) or n > 0

        def steps(eng, slots):
            for i in range(LOOP_FROM):
                slots(i, i % RING)
            with eng.Fori(LOOP_FROM, LOOP_TO - RING + 1, RING) as i:
                for r in range(RING):
                    slots(i + r if r else i, (LOOP_FROM + r) % RING)
            for i in range(LOOP_TO, STEPS):
                slots(i, i % RING)

        def live(b):
            return not isinstance(b, int) or 0 <= b < NB

        def due(i, s, name):
            lag, slot = WHEN[name]
            return slot == s and live(i - lag)

        def lag(name):
            return WHEN[name][0]

        def turn(i, s, name, count, every=1):
            for n in range(count):
                l, slot = divmod(AT[name] + int(every * n), SLOTS)
                if slot == s and live(i - l):
                    yield l, n

        @block.sync
        def _(sp):
            sp.dma_start(wqkv_sb[:], w_qkv).then_inc(wqkv_load, DMA)

            def load_weights():
                sp.dma_start(wr_sb[:], Wr).then_inc(w_load, DMA)
                sp.dma_start(wg_sb[:, 4, :], Sg).then_inc(w_load, DMA)
                sp.dma_start(wu_sb[:, 4, :], Su).then_inc(w_load, DMA)
                sp.dma_start(wd_sb[:, 4, :], Sd).then_inc(w_load, DMA)
                for e2 in range(2):
                    es = slice(4 * e2, 4 * e2 + 4)
                    half = slice(F * e2, F * e2 + F)
                    sp.dma_start(wg_sb[:, 0:4, half], Wg[es].rearrange("c d f -> d c f")).then_inc(w_load, DMA)
                    sp.dma_start(wu_sb[:, 0:4, half], Wu[es].rearrange("c d f -> d c f")).then_inc(w_load, DMA)
                    sp.dma_start(wd_sb[half, 0:4, :], Wd[es].rearrange("c f d -> f c d")).then_inc(w_load, DMA)
                for t in range(TT):
                    sp.dma_start(bias_sb[:, t, :], bias.rearrange("(a e) -> a e", a=1).broadcast_to([P, E])).then_inc(w_load, DMA)
                for gj in range(8):
                    for u in range(2):
                        sp.dma_start(wout_sb[16 * gj + 8 * u:16 * gj + 8 * u + 8, :],
                                     w_out[64 * u + 8 * gj:64 * u + 8 * gj + 8, :]).then_inc(w_load, DMA)

            def slots(i, r):
                for s in range(SLOTS):
                    if due(i, s, "load_x"):
                        b = i
                        if some(n_wait := count(TT, b)):
                            sp.wait_ge(applied[1], n_wait)
                        sp.dma_start(x_sb[:], x[b].rearrange("(t p) d -> p t d", p=P)).then_inc(x_load, DMA)
                        if isinstance(i, int) and i == 0:
                            load_weights()
                    if due(i, s, "spill"):
                        b = i - lag("spill")
                        sp.wait_ge(part3_done, count(1, b, 1))
                        sp.dma_start(qk_dram[r].rearrange("a u d x n -> (u d x) a n"), parts[:]).then_inc(qk_spilled, DMA)
                    for l, m in turn(i, s, "stack", 6, STACK_EVERY):
                        b = i - l
                        rb = (r - l) % RING
                        u, n = m // 3, m % 3
                        row = 64 * u + 8 * sum(copies for _, copies in PARTS_Q[:n])
                        if m == 0 and isinstance(b, int) and live(b - 1):
                            sp.wait_ge(s1_done, count(H, b - 1, 1))
                        if m == 0:
                            if some(n_wait := count(H, b - 2)):
                                sp.wait_ge(s2_done, n_wait)
                            sp.wait_ge(qk_spilled, count(DMA, b, DMA))
                        first, copies = PARTS_Q[n]
                        src = qk_dram[rb][2 * first:2 * (first + copies):2, u].rearrange("a d x n -> a d (x n)")
                        sp.dma_start(qs[rb][row:row + 8 * copies], src).then_inc(qk_stacked, DMA)
                        first, copies = PARTS_K[n]
                        src = qk_dram[rb][2 * first + 1:2 * first + 2, u].rearrange("a d x n -> a d (x n)").broadcast_to([copies, DH, 8 * N])
                        sp.dma_start(ks[rb][row:row + 8 * copies], src).then_inc(qk_stacked, DMA)
                    if due(i, s, "max_spill"):
                        b = i - lag("max_spill")
                        if isinstance(b, int) and b > 0:
                            sp.wait_ge(max_stacked, count(2 * DMA, b))
                        sp.wait_ge(max3_done, count(1, b, 1))
                        sp.dma_start(max_dram.rearrange("a h n -> h a n"), mparts[:]).then_inc(max_spilled, DMA)
                    if due(i, s, "max_stack"):
                        b = i - lag("max_stack")
                        sp.wait_ge(max_spilled, count(DMA, b, DMA))
                        q = qs[(r - lag("max_stack")) % RING]
                        for u in range(2):
                            sp.dma_start(q[64 * u + ROWS:64 * u + ROWS_MAX], max_dram[:, 8 * u:8 * u + 8, :]).then_inc(max_stacked, DMA)
                    for g in range(2):
                        if due(i, s, f"pv_spill{g}"):
                            b = i - lag(f"pv_spill{g}")
                            if isinstance(b, int) and b > 0:
                                sp.wait_ge(pv_loaded, count(2 * DMA, b))
                            sp.wait_ge(pv_copied, count(2, b, g + 1))
                            sp.dma_start(pv_dram[g], pv_sb[:, g, :]).then_inc(pv_spilled, DMA)
                    if due(i, s, "pv_load"):
                        b = i - lag("pv_load")
                        if isinstance(b, int) and b > 0:
                            sp.wait_ge(norm_done, count(1, b))
                        sp.wait_ge(pv_spilled, count(2 * DMA, b, 2 * DMA))
                        rows = pv_dram.rearrange("g (j k) n -> (g j) k n", k=32)
                        sp.dma_start(oc[:], rows[:, 0:16, :]).then_inc(pv_loaded, DMA)
                        sp.dma_start(den[:], rows[:, 16:32, :]).then_inc(pv_loaded, DMA)
                    if due(i, s, "load_x2"):
                        b = i - lag("load_x2")
                        if some(n_wait := count(1, b)):
                            sp.wait_ge(add2_done, n_wait)
                        sp.dma_start(x_res[:], x[b].rearrange("(t p) d -> p t d", p=P)).then_inc(x_res_load, DMA)
                    if due(i, s, "w_spill"):
                        b = i - lag("w_spill")
                        if isinstance(b, int) and b > 0:
                            sp.wait_ge(rw_loaded, count(2 * DMA, b))
                        sp.wait_ge(wT_copied, count(1, b, 1))
                        sp.dma_start(rw_dram, rwT[:]).then_inc(rw_spilled, DMA)
                    if due(i, s, "w_load"):
                        b = i - lag("w_load")
                        if isinstance(b, int) and b > 0:
                            sp.wait_ge(hw_done, count(4, b))
                        sp.wait_ge(rw_spilled, count(DMA, b, DMA))
                        for e2 in range(2):
                            src = rw_dram[4 * e2:4 * e2 + 4].rearrange("(a c) n -> a (c n)", a=1).broadcast_to([F, 4 * N])
                            sp.dma_start(rwb[F * e2:F * e2 + F].rearrange("p c n -> p (c n)"), src).then_inc(rw_loaded, DMA)
                    if due(i, s, "store"):
                        b = i - lag("store")
                        sp.wait_ge(add4_done, count(1, b, 1))
                        sp.dma_start(out[b].rearrange("(t p) d -> p t d", p=P), x4[:]).then_inc(stored, DMA)

            steps(sp, slots)
            sp.wait_ge(stored, DMA * NB)

        @block.tensor
        def _(pe):
            pe.wait_ge(consts, 3)
            pe.wait_ge(wqk_done, 2)

            def s1(b, r, k):
                h = head_of(k)
                row = 64 * (h // 8)
                if k == 0:
                    pe.wait_ge(qk_stacked, count(12 * DMA, b, 12 * DMA))
                    pe.wait_ge(ones_done, 1) if isinstance(b, int) and b == 0 else None
                if some(n_wait := count(H, b, k - 1)):
                    pe.wait_ge(max_done, n_wait)
                for c in range(TT):
                    mm = pe.matmul(s1p[k % 2][:, c, :], qs[r][row:row + ROWS, h % 8, c * P:(c + 1) * P],
                                   ks[r][row:row + ROWS, h % 8, :], start=True, stop=True)
                mm.then_inc(s1_done, 1)

            def s2(b, r, k):
                h = head_of(k)
                row = 64 * (h // 8)
                if k == 0:
                    pe.wait_ge(max_stacked, count(2 * DMA, b, 2 * DMA))
                if some(n_wait := count(H, b, k - 1)):
                    pe.wait_ge(exp_done, n_wait)
                for c in range(TT):
                    mm = pe.matmul(s2p[k % 2][:, c, :], ks[r][row:row + ROWS_MAX, h % 8, c * P:(c + 1) * P],
                                   qs[r][row:row + ROWS_MAX, h % 8, :], start=True, stop=True)
                mm.then_inc(s2_done, 1)

            def pv(b, r, g, n):
                u, c = n // TT, n % TT
                if n == 0:
                    pe.wait_ge(exp_done, count(H, b, 8 * g + 8))
                    pe.wait_ge(v_copied, count(1, b, 1))
                    if some(n_wait := count(2, b, g)):
                        pe.wait_ge(pv_copied, n_wait)
                for j in range(4):
                    k = 8 * g + 2 * j + u
                    mm = pe.matmul(pvp[32 * j:32 * j + 32, 0:N], va[r][:, c, k, :], pr[:, k, c * N:(c + 1) * N],
                                   start=(n == 0), stop=(n == 3))
                if n == 3:
                    mm.then_inc(pv_done, 1)

            def slots(i, r):
                for s in range(SLOTS):
                    if due(i, s, "maxT"):
                        b = i - lag("maxT")
                        pe.wait_ge(max_done, count(H, b, H))
                        pe.wait_ge(v_copied, count(1, b + 1, 1))
                        if not live(b + 1) and live(b - 4):
                            pe.wait_ge(wT_copied, count(1, b - 4, 1))
                        for c in range(TT):
                            mm = pe.transpose(bank_a[0:H, c * P:(c + 1) * P], mx[(r - lag("maxT")) % RING][:, c, :], ident[:])
                        mm.then_inc(maxT_done, 1)
                    for l, k in turn(i, s, "s1", H):
                        s1(i - l, (r - l) % RING, k)
                    for l, k in turn(i, s, "s2", H):
                        s2(i - l, (r - l) % RING, k)
                    for g in range(2):
                        for l, n in turn(i, s, f"pv{g}", 4, PV_EVERY):
                            pv(i - l, (r - l) % RING, g, n)
                    if due(i, s, "xT"):
                        b = i
                        pe.wait_ge(applied[1], count(TT, b, TT))
                        if live(b - 6):
                            pe.wait_ge(wT_copied, count(1, b - 6, 1))
                        elif live(b - 3):
                            pe.wait_ge(max_rest_done, count(1, b - 3, 1))
                        elif live(b - 2):
                            pe.wait_ge(v_copied, count(1, b - 2, 1))
                        elif live(b - 1):
                            pe.wait_ge(rest1_done, count(1, b - 1, 1))
                        for c in range(TT):
                            mm = pe.transpose(bank_a[:, c * P:(c + 1) * P], xn[:, c, :], ident[:])
                        mm.then_inc(xT_done, 1)
                    if due(i, s, "qk"):
                        pe.wait_ge(xT_copied, count(1, i, 1))
                        for n in range(2):
                            mm = pe.matmul(bank_a[:, n * N:(n + 1) * N], wqk_sb[:, n, :], xT[r][:], start=True, stop=True)
                        mm.then_inc(qk_done, 1)
                    if due(i, s, "v"):
                        b = i - lag("v")
                        x_T = xT[(r - lag("v")) % RING]
                        pe.wait_ge(rest1_done, count(1, b + 1, 1))
                        if not live(b + 1) and live(b - 5):
                            pe.wait_ge(wT_copied, count(1, b - 5, 1))
                        for c in range(TT):
                            mm = pe.matmul(bank_a[:, c * P:(c + 1) * P], x_T[:, c * P:(c + 1) * P],
                                           wqkv_sb[:, 2 * D:3 * D].rearrange("p (u x d) -> p x u d", u=2, x=8),
                                           start=True, stop=True)
                        mm.then_inc(v_done, 1)
                    if due(i, s, "proj"):
                        b = i - lag("proj")
                        if isinstance(b, int) and b == 0:
                            pe.wait_ge(w_load, DMA * 28)
                        pe.wait_ge(norm_done, count(1, b, 1))
                        if some(n_wait := count(1, b - 1)):
                            pe.wait_ge(down_copied, n_wait)
                        for c in range(TT):
                            mm = pe.matmul(bank_d[0][:, c * P:(c + 1) * P], on[:, c * P:(c + 1) * P], wout_sb[:],
                                           start=True, stop=True)
                        mm.then_inc(proj_done, 1)
                    if due(i, s, "x3T"):
                        b = i - lag("x3T")
                        pe.wait_ge(applied[3], count(TT, b, TT))
                        if some(n_wait := count(CHUNKS, b)):
                            pe.wait_ge(h_done, n_wait)
                        for c in range(TT):
                            mm = pe.transpose(bank_d[1][:, c * P:(c + 1) * P], x3[:, c, :], ident[:])
                        mm.then_inc(x3T_done, 1)
                    if due(i, s, "router"):
                        b = i - lag("router")
                        pe.wait_ge(x3T_copied, count(1, b, 1))
                        for c in range(TT):
                            mm = pe.matmul(bank_d[1][:, c * E:(c + 1) * E], x3T[:, c * P:(c + 1) * P], wr_sb[:],
                                           start=True, stop=True)
                        mm.then_inc(router_done, 1)
                    for n in range(CHUNKS):
                        if due(i, s, f"gu{n}"):
                            b = i - lag(f"gu{n}")
                            c = ORDER[n]
                            if n == 0:
                                pe.wait_ge(logits_done, count(1, b, 1))
                            elif n == 1:
                                pe.wait_ge(proj_copied, count(1, b + 1, 1))
                                if not live(b + 1):
                                    pe.wait_ge(down_copied, count(1, b))
                            else:
                                pe.wait_ge(h_done, count(CHUNKS, b, n - 1))
                            bank = bank_d[BANK[n]]
                            pe.matmul(bank[:, 0:N], wg_sb[:, c, :], x3T[:], start=True, stop=True)
                            pe.matmul(bank[:, N:2 * N], wu_sb[:, c, :], x3T[:], start=True, stop=True).then_inc(gu_done, 1)
                    if due(i, s, "wT"):
                        b = i - lag("wT")
                        pe.wait_ge(rw_done, count(1, b, 1))
                        pe.wait_ge(max_rest_done, count(1, b + 3, 1))
                        for c in range(TT):
                            mm = pe.transpose(bank_a[0:E, c * P:(c + 1) * P], rw[:, c, :], ident[:])
                        mm.then_inc(wT_done, 1)
                    for c in range(TT):
                        if due(i, s, f"down{c}"):
                            b = i - lag(f"down{c}")
                            if c == 0:
                                pe.wait_ge(hw_done, count(4, b, 4))
                                pe.wait_ge(h_done, count(CHUNKS, b, CHUNKS))
                            for n in range(CHUNKS):
                                src = hw[:, n, c * P:(c + 1) * P] if n < 4 else hb[:, 4, c * P:(c + 1) * P]
                                mm = pe.matmul(bank_d[0][:, c * P:(c + 1) * P], src, wd_sb[:, n, :],
                                               start=(n == 0), stop=(n == CHUNKS - 1))
                            if c == TT - 1:
                                mm.then_inc(down_done, 1)

            steps(pe, slots)

        @block.scalar
        def _(act):
            def slots(i, r):
                for s in range(SLOTS):
                    for l, k in turn(i, s, "s2", H):
                        b = i - l
                        act.wait_ge(s2_done, count(H, b, k + 1))
                        if some(n_wait := count(2, b - 1, k // 8 + 1)):
                            act.wait_ge(pv_done, n_wait)
                        nc.scalar.activation(pr[:, k, :], s2p[k % 2][:].rearrange("p c n -> p (c n)"),
                                             ACT.Exp, scale=SCALE).then_inc(exp_done, 1)
                    if due(i, s, "max1"):
                        b = i - lag("max1")
                        act.wait_ge(maxT_done, count(1, b, 1))
                        if some(n_wait := count(DMA, b)):
                            act.wait_ge(max_spilled, n_wait)
                        nc.scalar.activation(mparts[:, 0, :], bank_a[0:H, 0:N], ACT.Copy, scale=-1.0).then_inc(max1_done, 1)
                    if due(i, s, "max2"):
                        b = i - lag("max2")
                        act.wait_ge(max_rest_done, count(1, b, 1))
                        if some(n_wait := count(DMA, b)):
                            act.wait_ge(max_spilled, n_wait)
                        nc.scalar.copy(mparts[:, 1, :], mrest[:]).then_inc(max2_done, 1)
                    if due(i, s, "xT_copy"):
                        act.wait_ge(xT_done, count(1, i, 1))
                        if some(n_wait := count(1, i - 2)):
                            act.wait_ge(v_done, n_wait)
                        nc.scalar.copy(xT[r][:], bank_a[:, 0:N]).then_inc(xT_copied, 1)
                    if due(i, s, "part1"):
                        act.wait_ge(qk_done, count(1, i, 1))
                        if some(n_wait := count(DMA, i)):
                            act.wait_ge(qk_spilled, n_wait)
                        nc.scalar.copy(parts[:, 0:2, :].rearrange("p a n -> p (a n)"), bank_a[:]).then_inc(part1_done, 1)
                    if due(i, s, "part2"):
                        act.wait_ge(rest1_done, count(1, i, 1))
                        nc.scalar.copy(parts[:, 2:4, :].rearrange("p a n -> p (a n)"), rest[:]).then_inc(part2_done, 1)
                    if due(i, s, "v_copy"):
                        b = i - lag("v_copy")
                        act.wait_ge(v_done, count(1, b, 1))
                        if some(n_wait := count(2, b - 2)):
                            act.wait_ge(pv_done, n_wait)
                        dst = va[(r - lag("v_copy")) % RING][:].rearrange("p c (x u) k -> p (c x) (u k)", u=2)
                        for u in range(2):
                            cp = nc.scalar.copy(dst[:, :, 40 * u:40 * u + DH],
                                                bank_a[:, 0:N].rearrange("p (x u d) -> p x u d", u=2, d=DH)[:, :, u, :])
                        cp.then_inc(v_copied, 1)
                    for g in range(2):
                        if due(i, s, f"pv_copy{g}"):
                            b = i - lag(f"pv_copy{g}")
                            act.wait_ge(pv_done, count(2, b, g + 1))
                            if some(n_wait := count(2 * DMA, b - 1, DMA * (g + 1))):
                                act.wait_ge(pv_spilled, n_wait)
                            nc.scalar.copy(pv_sb[:, g, :], pvp[:, 0:N]).then_inc(pv_copied, 1)
                    if due(i, s, "proj_copy"):
                        b = i - lag("proj_copy")
                        act.wait_ge(proj_done, count(1, b, 1))
                        if some(n_wait := count(TT, b)):
                            act.wait_ge(applied[2], n_wait)
                        nc.scalar.copy(proj[:].rearrange("p t d -> p (t d)"), bank_d[0][:, 0:N]).then_inc(proj_copied, 1)
                    if due(i, s, "down_copy"):
                        b = i - lag("down_copy")
                        act.wait_ge(down_done, count(1, b, 1))
                        if some(n_wait := count(TT, b)):
                            act.wait_ge(applied[4], n_wait)
                        nc.scalar.copy(down[:].rearrange("p t d -> p (t d)"), bank_d[0][:, 0:N]).then_inc(down_copied, 1)
                    if due(i, s, "x3T_copy"):
                        b = i - lag("x3T_copy")
                        act.wait_ge(x3T_done, count(1, b, 1))
                        if some(n_wait := count(CHUNKS, b)):
                            act.wait_ge(gu_done, n_wait)
                        nc.scalar.copy(x3T[:], bank_d[1][:, 0:N]).then_inc(x3T_copied, 1)
                    for n in range(CHUNKS):
                        if due(i, s, f"tanh{n}"):
                            b = i - lag(f"tanh{n}")
                            act.wait_ge(gu_done, count(CHUNKS, b, n + 1))
                            if some(n_wait := count(CHUNKS, b, n - 1)):
                                act.wait_ge(ha_done, n_wait)
                            nc.scalar.activation(th[:, n % 2, :], bank_d[BANK[n]][:, 0:N], ACT.Tanh, scale=0.5).then_inc(tanh_done, 1)
                    if due(i, s, "gate_exp"):
                        b = i - lag("gate_exp")
                        act.wait_ge(gd_done, count(1, b, 1))
                        if some(n_wait := count(1, b)):
                            act.wait_ge(gp2_done, n_wait)
                        nc.scalar.activation(ge[:], gd[:], ACT.Exp).then_inc(gexp_done, 1)
                    if due(i, s, "wT_copy"):
                        b = i - lag("wT_copy")
                        act.wait_ge(wT_done, count(1, b, 1))
                        if some(n_wait := count(DMA, b)):
                            act.wait_ge(rw_spilled, n_wait)
                        nc.scalar.copy(rwT[:], bank_a[0:E, 0:N]).then_inc(wT_copied, 1)

            steps(act, slots)

        @block.vector
        def _(dve):
            for r in range(RING):
                nc.vector.memset(ks[r][:], 1.0)
            nc.vector.memset(eps[:], EPS)
            nc.vector.memset(mhalf[:], -0.5).then_inc(consts, 1)
            for r in range(RING):
                nc.vector.memset(va[r][:], 0.0).then_inc(zeroed, 1)
            dve.wait_ge(zeroed, RING)
            for r in range(RING):
                dst = va[r][:].rearrange("p c (x u) k -> p (c x) (u k)", u=2)
                for u in range(2):
                    one = nc.vector.memset(dst[:, :, 40 * u + 16:40 * u + 24], 1.0)
            one.then_inc(ones_done, 1)
            dve.wait_ge(wqkv_load, DMA)
            for n in range(2):
                nc.vector.tensor_copy(wqk_sb[:, n, :].rearrange("p (u d x) -> p u d x", u=2, d=DH),
                                      wqkv_sb[:, n * D:(n + 1) * D].rearrange("p (u x d) -> p u d x", u=2, x=8)).then_inc(wqk_done, 1)
            dve.wait_ge(iota_i_done, 1)
            nc.vector.tensor_copy(iota[:], iota_i[:]).then_inc(consts, 1)

            def stats(L, b, tiles):
                if some(n_wait := count(TT, b)):
                    dve.wait_ge(aggr_done[L], n_wait)
                for t in range(TT):
                    nc.vector.bn_stats(st[L][:, t, :], tiles(t)).then_inc(stats_done[L], 1)

            def apply(L, b, dst, tiles):
                dve.wait_ge(rstd_done[L], count(1, b, 1))
                for t in range(TT):
                    nc.vector.tensor_scalar(dst[:, t, :], tiles(t), mv[L][:, t, 0:1], rs[L][:, t:t + 1],
                                            ALU.subtract, ALU.mult).then_inc(applied[L], 1)

            def slots(i, r):
                for s in range(SLOTS):
                    if due(i, s, "max_rest"):
                        b = i - lag("max_rest")
                        dve.wait_ge(max1_done, count(1, b, 1))
                        if some(n_wait := count(1, b)):
                            dve.wait_ge(max3_done, n_wait)
                        nc.vector.scalar_tensor_tensor(out=mrest[:], in0=bank_a[0:H, 0:N], scalar=-1.0, in1=mparts[:, 0, :],
                                                       op0=ALU.mult, op1=ALU.subtract).then_inc(max_rest_done, 1)
                    for L in (1, 2, 3, 4):
                        if due(i, s, f"aggr{L}"):
                            b = i - lag(f"aggr{L}")
                            dve.wait_ge(stats_done[L], count(TT, b, TT))
                            if some(n_wait := count(TT, b)):
                                dve.wait_ge(applied[L], n_wait)
                    for l, k in turn(i, s, "s1", H):
                        b = i - l
                        dve.wait_ge(s1_done, count(H, b, k + 1))
                        if k == 0:
                            if some(n_wait := count(1, b - 2)):
                                dve.wait_ge(maxT_done, n_wait)
                        nc.vector.tensor_reduce(mx[(r - l) % RING][:, :, head_of(k)], s1p[k % 2][:], AX.X, ALU.max).then_inc(max_done, 1)
                    for L in (1, 2, 3, 4):
                        if due(i, s, f"aggr{L}"):
                            for t in range(TT):
                                nc.vector.bn_aggr(mv[L][:, t, :], st[L][:, t, :]).then_inc(aggr_done[L], 1)
                    if due(i, s, "stats1"):
                        dve.wait_ge(x_load, count(DMA, i, DMA))
                        stats(1, i, lambda t: x_sb[:, t, :])
                    if due(i, s, "apply1"):
                        if some(n_wait := count(1, i)):
                            dve.wait_ge(xT_done, n_wait)
                        apply(1, i, xn, lambda t: x_sb[:, t, :])
                    if due(i, s, "rest1"):
                        b = i
                        dve.wait_ge(part1_done, count(1, b, 1))
                        if some(n_wait := count(1, b)):
                            dve.wait_ge(part3_done, n_wait)
                        nc.vector.tensor_tensor(rest[:], bank_a[:], parts[:, 0:2, :].rearrange("p a n -> p (a n)"),
                                                ALU.subtract).then_inc(rest1_done, 1)
                    if due(i, s, "recip"):
                        b = i - lag("recip")
                        dve.wait_ge(pv_loaded, count(2 * DMA, b, 2 * DMA))
                        if some(n_wait := count(1, b)):
                            dve.wait_ge(norm_done, n_wait)
                        nc.vector.reciprocal(rden[:], den[:]).then_inc(recip_done, 1)
                    if due(i, s, "stats2"):
                        b = i - lag("stats2")
                        dve.wait_ge(proj_copied, count(1, b, 1))
                        stats(2, b, lambda t: proj[:, t, :])
                    if due(i, s, "apply2"):
                        b = i - lag("apply2")
                        if some(n_wait := count(1, b)):
                            dve.wait_ge(add2_done, n_wait)
                        apply(2, b, y2, lambda t: proj[:, t, :])
                    if due(i, s, "stats3"):
                        b = i - lag("stats3")
                        x2b = x2[(r - lag("stats3")) % RING]
                        dve.wait_ge(add2_done, count(1, b, 1))
                        stats(3, b, lambda t: x2b[:, t, :])
                    if due(i, s, "apply3"):
                        b = i - lag("apply3")
                        x2b = x2[(r - lag("apply3")) % RING]
                        if some(n_wait := count(1, b)):
                            dve.wait_ge(x3T_done, n_wait)
                        apply(3, b, x3, lambda t: x2b[:, t, :])
                    if due(i, s, "top"):
                        b = i - lag("top")
                        dve.wait_ge(router_done, count(1, b, 1))
                        if some(n_wait := count(TT, b)):
                            dve.wait_ge(topi_done, n_wait)
                        nc.vector.tensor_tensor(lg[:].rearrange("p t e -> p (t e)"), bank_d[1][:, 0:TT * E],
                                                bias_sb[:].rearrange("p t e -> p (t e)"), ALU.add).then_inc(logits_done, 1)
                        dve.wait_ge(consts, 3)
                        dve.wait_ge(logits_done, count(1, b, 1))
                        if some(n_wait := count(1, b)):
                            dve.wait_ge(gd_done, n_wait)
                        for t in range(TT):
                            nc.vector.max(top_v[:, t, :], lg[:, t, :]).then_inc(topv_done, 1)
                        dve.wait_ge(topv_done, count(TT, b, TT))
                        if some(n_wait := count(1, b)):
                            dve.wait_ge(gexp_done, n_wait)
                        nc.vector.tensor_tensor(gd[:], top_v[:, :, 1], top_v[:, :, 0], ALU.subtract).then_inc(gd_done, 1)
                        dve.wait_ge(consts, 3)
                        if some(n_wait := count(1, b)):
                            dve.wait_ge(topf_done, n_wait)
                        for t in range(TT):
                            nc.vector.max_index(top_i[:, t, :], top_v[:, t, :], lg[:, t, :]).then_inc(topi_done, 1)
                        dve.wait_ge(topi_done, count(TT, b, TT))
                        if some(n_wait := count(2 * TT, b)):
                            dve.wait_ge(wa_done, n_wait)
                        nc.vector.tensor_copy(top_f[:], top_i[:, :, 0:2]).then_inc(topf_done, 1)
                    if due(i, s, "gates"):
                        b = i - lag("gates")
                        dve.wait_ge(gexp_done, count(1, b, 1))
                        if some(n_wait := count(1, b)):
                            dve.wait_ge(gp1_done, n_wait)
                        nc.vector.tensor_scalar(g1[:], ge[:], 1.0, None, ALU.add).then_inc(g1_done, 1)
                        dve.wait_ge(g1_done, count(1, b, 1))
                        if some(n_wait := count(2 * TT, b)):
                            dve.wait_ge(wa_done, n_wait)
                        nc.vector.reciprocal(gp[:, 0, :], g1[:]).then_inc(gp1_done, 1)
                        dve.wait_ge(gp1_done, count(1, b, 1))
                        nc.vector.tensor_tensor(gp[:, 1, :], gp[:, 0, :], ge[:], ALU.mult).then_inc(gp2_done, 1)
                        dve.wait_ge(gp2_done, count(1, b, 1))
                        dve.wait_ge(topf_done, count(1, b, 1))
                        if some(n_wait := count(1, b)):
                            dve.wait_ge(rw_done, n_wait)
                        for a in range(2):
                            for t in range(TT):
                                nc.vector.tensor_scalar(wa[:, a, t, :], iota[:], top_f[:, t, a:a + 1], gp[:, a, t:t + 1],
                                                        ALU.is_equal, ALU.mult).then_inc(wa_done, 1)
                    for n in range(CHUNKS):
                        if due(i, s, f"h{n}"):
                            b = i - lag(f"h{n}")
                            bank = bank_d[BANK[n]]
                            dve.wait_ge(tanh_done, count(CHUNKS, b, n + 1))
                            if some(n_wait := count(CHUNKS, b, n - 1)):
                                dve.wait_ge(h_done, n_wait)
                            nc.vector.scalar_tensor_tensor(out=ha[:, n % 2, :], in0=th[:, n % 2, :], scalar=1.0, in1=bank[:, 0:N],
                                                           op0=ALU.add, op1=ALU.mult).then_inc(ha_done, 1)
                            dve.wait_ge(ha_done, count(CHUNKS, b, n + 1))
                            if some(n_wait := count(1, b)):
                                dve.wait_ge(down_done, n_wait)
                            nc.vector.scalar_tensor_tensor(out=hb[:, ORDER[n], :], in0=ha[:, n % 2, :], scalar=0.5, in1=bank[:, N:2 * N],
                                                           op0=ALU.mult, op1=ALU.mult).then_inc(h_done, 1)
                    if due(i, s, "stats4"):
                        b = i - lag("stats4")
                        dve.wait_ge(down_copied, count(1, b, 1))
                        stats(4, b, lambda t: down[:, t, :])
                    if due(i, s, "apply4"):
                        b = i - lag("apply4")
                        if some(n_wait := count(1, b)):
                            dve.wait_ge(add4_done, n_wait)
                        apply(4, b, y4, lambda t: down[:, t, :])

            steps(dve, slots)

        @block.gpsimd
        def _(pool):
            nc.gpsimd.memset(ident[:], 0.0).then_inc(ident_zeroed, 1)
            pool.wait_ge(ident_zeroed, 1)
            nc.gpsimd.affine_select(out=ident[:], in_=ident[:], compare_op=ALU.not_equal, fill=1.0, base=0,
                                    pattern=[[-1, P]], channel_multiplier=1).then_inc(consts, 1)
            nc.gpsimd.iota(iota_i[:], pattern=[[1, E]], base=0, channel_multiplier=0).then_inc(iota_i_done, 1)
            pool.wait_ge(consts, 3)

            def rstd(L, b):
                pool.wait_ge(aggr_done[L], count(TT, b, TT))
                if some(n_wait := count(1, b)):
                    pool.wait_ge(rstd_done[L], n_wait)
                nc.gpsimd.tensor_tensor(vareps[L][:], mv[L][:, :, 1], eps[:], ALU.add).then_inc(vareps_done[L], 1)
                pool.wait_ge(vareps_done[L], count(1, b, 1))
                if some(n_wait := count(TT, b)):
                    pool.wait_ge(applied[L], n_wait)
                nc.gpsimd.tensor_tensor(rs[L][:], vareps[L][:], mhalf[:], ALU.pow).then_inc(rstd_done[L], 1)

            def flat(tile):
                return tile[:].rearrange("p t d -> p (t d)")

            def slots(i, r):
                for s in range(SLOTS):
                    for L in (1, 2, 3, 4):
                        if due(i, s, f"rstd{L}"):
                            rstd(L, i - lag(f"rstd{L}"))
                    if due(i, s, "max3"):
                        b = i - lag("max3")
                        pool.wait_ge(max2_done, count(1, b, 1))
                        if some(n_wait := count(DMA, b)):
                            pool.wait_ge(max_spilled, n_wait)
                        nc.gpsimd.tensor_tensor(mparts[:, 2, :], mrest[:], mparts[:, 1, :], ALU.subtract).then_inc(max3_done, 1)
                    if due(i, s, "part3"):
                        b = i
                        pool.wait_ge(part2_done, count(1, b, 1))
                        if some(n_wait := count(DMA, b)):
                            pool.wait_ge(qk_spilled, n_wait)
                        nc.gpsimd.tensor_tensor(parts[:, 4:6, :].rearrange("p a n -> p (a n)"), rest[:],
                                                parts[:, 2:4, :].rearrange("p a n -> p (a n)"), ALU.subtract).then_inc(part3_done, 1)
                    if due(i, s, "norm"):
                        b = i - lag("norm")
                        pool.wait_ge(recip_done, count(1, b, 1))
                        if some(n_wait := count(1, b)):
                            pool.wait_ge(proj_done, n_wait)
                        nc.gpsimd.tensor_tensor(on[:], oc[:], rden[:], ALU.mult).then_inc(norm_done, 1)
                    if due(i, s, "add2"):
                        b = i - lag("add2")
                        pool.wait_ge(applied[2], count(TT, b, TT))
                        pool.wait_ge(x_res_load, count(DMA, b, DMA))
                        if some(n_wait := count(1, b - 2)):
                            pool.wait_ge(add4_done, n_wait)
                        nc.gpsimd.tensor_tensor(flat(x2[(r - lag("add2")) % RING]), flat(y2), flat(x_res), ALU.add).then_inc(add2_done, 1)
                    if due(i, s, "weights"):
                        b = i - lag("weights")
                        pool.wait_ge(wa_done, count(2 * TT, b, 2 * TT))
                        if some(n_wait := count(1, b)):
                            pool.wait_ge(wT_done, n_wait)
                        nc.gpsimd.tensor_tensor(flat(rw), wa[:, 0].rearrange("p t e -> p (t e)"),
                                                wa[:, 1].rearrange("p t e -> p (t e)"), ALU.add).then_inc(rw_done, 1)
                    for n in range(4):
                        if due(i, s, f"hw{n}"):
                            b = i - lag(f"hw{n}")
                            if n == 0:
                                pool.wait_ge(rw_loaded, count(2 * DMA, b, 2 * DMA))
                                if some(n_wait := count(1, b)):
                                    pool.wait_ge(down_done, n_wait)
                            pool.wait_ge(h_done, count(CHUNKS, b, n + 2))
                            nc.gpsimd.tensor_tensor(hw[:, n, :], hb[:, n, :], rwb[:, n, :], ALU.mult).then_inc(hw_done, 1)
                    if due(i, s, "add4"):
                        b = i - lag("add4")
                        pool.wait_ge(applied[4], count(TT, b, TT))
                        if some(n_wait := count(DMA, b)):
                            pool.wait_ge(stored, n_wait)
                        nc.gpsimd.tensor_tensor(flat(x4), flat(y4), flat(x2[(r - lag("add4")) % RING]), ALU.add).then_inc(add4_done, 1)

            steps(pool, slots)


_INS = ["L0_attn_x", "L0_attn_w_qkv", "L0_attn_w_out", "L0_ffn_Wr", "L0_ffn_Wg", "L0_ffn_Wu", "L0_ffn_Wd",
        "L0_ffn_Sg", "L0_ffn_Su", "L0_ffn_Sd", "L0_ffn_expert_bias"]


def kernel(**inputs):
    import numpy as _np
    import concourse.bacc as _bacc
    from concourse import mybir as _mybir
    from concourse.bass_utils import run_bass_kernel_spmd as _run

    nc = _bacc.Bacc("TRN2", target_bir_lowering=False, num_devices=1)
    arrays, args = {}, []
    for name in _INS:
        a = _np.ascontiguousarray(inputs[name])
        arrays[f"in_{name}_dram"] = a
        args.append(nc.dram_tensor(f"in_{name}_dram", a.shape, _mybir.dt.from_np(a.dtype), kind="ExternalInput").ap())
    shape = inputs["L0_attn_x"].shape
    args.append(nc.dram_tensor("out_0_dram", shape, _mybir.dt.float32, kind="ExternalOutput").ap())
    sandwich(nc, *args)
    r = _run(nc, [arrays], core_ids=[0])
    return r.results[0]["out_0_dram"]
```
